# Optimizing a Trainium2 kernel written in Bass

```python
import numpy as np
import jax
import jax.numpy as jnp

def _softmax(x, axis=-1):
    return jax.nn.softmax(x, axis=axis)

def _gelu(x):
    return jax.nn.gelu(x, approximate=True)

def _silu(x):
    return jax.nn.silu(x)

def _sigmoid(x):
    return jax.nn.sigmoid(x)

def _layernorm(x, axis=-1, eps=1e-05):
    m = jnp.mean(x, axis=axis, keepdims=True)
    v = jnp.var(x, axis=axis, keepdims=True)
    return (x - m) / jnp.sqrt(v + eps)

def _scatter_add(tgt, idx, src, axis=0):
    return tgt.at[idx].add(src)

def _segment_sum(src, seg, n):
    return jax.ops.segment_sum(src, seg, n)
kernel_name = 'mk_gnn_resnorm_d2_gnn_r8_35789e'

def setup_inputs(seed: int=0):
    np.random.seed(seed)
    _w = jnp.asarray

    def _rec_inputs():
        import jax
        import jax.numpy as jnp
        _gk = jax.random.key(seed)
        x = -0.000202 + 1 * jax.random.normal(jax.random.fold_in(_gk, 1), (6250, 128), jnp.float32)
        _s = jax.random.randint(jax.random.fold_in(_gk, 2), (100000,), 0, 6250, jnp.int32)
        _d = jax.random.randint(jax.random.fold_in(_gk, 3), (100000,), 0, 6250, jnp.int32)
        _loop = jnp.arange(6250, dtype=jnp.int32)
        src = jnp.concatenate([_s, _d, _loop])
        dst = jnp.concatenate([_d, _s, _loop])
        _o = jnp.argsort(dst, stable=True)
        src = src[_o]
        dst = dst[_o]
        return (x, src, dst)
    x, src, dst = _rec_inputs()

    def _L0_gnn_setup():
        import jax, jax.numpy as jnp
        import numpy as np
        N_NODES = 6250
        N_EDGES = 100000
        D_IN = 128
        U = 128
        H = 128
        key = jax.random.key(seed)
        ks = jax.random.split(key, 8)
        s = lambda d: 1.0 / np.sqrt(d)
        x = jax.random.normal(ks[0], (N_NODES, D_IN), dtype=jnp.float32)
        edge_index = jax.random.randint(ks[1], (2, N_EDGES), 0, N_NODES, dtype=jnp.int64)
        W1 = jax.random.normal(ks[2], (D_IN, U), dtype=jnp.float32) * s(D_IN)
        b1 = jax.random.normal(ks[3], (U,), dtype=jnp.float32) * 0.01
        W2 = jax.random.normal(ks[4], (2 * U, H), dtype=jnp.float32) * s(2 * U)
        b2 = jax.random.normal(ks[5], (H,), dtype=jnp.float32) * 0.01
        W3 = jax.random.normal(ks[6], (H, H), dtype=jnp.float32) * s(H)
        b3 = jax.random.normal(ks[7], (H,), dtype=jnp.float32) * 0.01
        return {'x': x, 'edge_index': edge_index, 'W1': W1, 'b1': b1, 'W2': W2, 'b2': b2, 'W3': W3, 'b3': b3}
    _L0_gnn_all = _L0_gnn_setup()
    _L0_gnn_in = {k: v for k, v in _L0_gnn_all.items() if k in ('W1', 'b1', 'W2', 'b2', 'W3', 'b3')}
    del _L0_gnn_all

    def _L1_gnn_setup():
        import jax, jax.numpy as jnp
        import numpy as np
        N = 6250
        E = 200000
        D = 128
        G = 128
        EPS = 1e-05
        NEG_SLOPE = 0.01
        key = jax.random.key(seed)
        ks = jax.random.split(key, 10)
        p = lambda k, sh: jax.random.normal(k, sh, dtype=jnp.float32) * 0.05
        return {'node_feats': jax.random.normal(ks[0], (N, D), dtype=jnp.float32), 'src': jax.random.randint(ks[1], (E,), 0, N, dtype=jnp.int32), 'dst': jax.random.randint(ks[2], (E,), 0, N, dtype=jnp.int32), 'we_dst': p(ks[3], (D,)), 'we_src': p(ks[4], (D,)), 'be': jnp.zeros((), jnp.float32), 'w_proj': p(ks[5], (D, G)), 'b_proj': jnp.zeros((G,), jnp.float32), 'w1': p(ks[6], (G + D, D)), 'b1': jnp.zeros((D,), jnp.float32), 'w2': p(ks[7], (D, D)), 'b2': jnp.zeros((D,), jnp.float32), 'gamma': jnp.ones((G,), jnp.float32), 'beta': jnp.zeros((G,), jnp.float32)}
    _L1_gnn_all = _L1_gnn_setup()
    _L1_gnn_in = {k: v for k, v in _L1_gnn_all.items() if k in ('we_dst', 'we_src', 'be', 'w_proj', 'b_proj', 'w1', 'b1', 'w2', 'b2', 'gamma', 'beta')}
    del _L1_gnn_all
    return {'x': x, 'src': src, 'dst': dst, 'L0_gnn_W1': _L0_gnn_in['W1'], 'L0_gnn_b1': _L0_gnn_in['b1'], 'L0_gnn_W2': _L0_gnn_in['W2'], 'L0_gnn_b2': _L0_gnn_in['b2'], 'L0_gnn_W3': _L0_gnn_in['W3'], 'L0_gnn_b3': _L0_gnn_in['b3'], 'L1_gnn_we_dst': _L1_gnn_in['we_dst'], 'L1_gnn_we_src': _L1_gnn_in['we_src'], 'L1_gnn_be': _L1_gnn_in['be'], 'L1_gnn_w_proj': _L1_gnn_in['w_proj'], 'L1_gnn_b_proj': _L1_gnn_in['b_proj'], 'L1_gnn_w1': _L1_gnn_in['w1'], 'L1_gnn_b1': _L1_gnn_in['b1'], 'L1_gnn_w2': _L1_gnn_in['w2'], 'L1_gnn_b2': _L1_gnn_in['b2'], 'L1_gnn_gamma': _L1_gnn_in['gamma'], 'L1_gnn_beta': _L1_gnn_in['beta']}

def reference(x, src, dst, L0_gnn_W1, L0_gnn_b1, L0_gnn_W2, L0_gnn_b2, L0_gnn_W3, L0_gnn_b3, L1_gnn_we_dst, L1_gnn_we_src, L1_gnn_be, L1_gnn_w_proj, L1_gnn_b_proj, L1_gnn_w1, L1_gnn_b1, L1_gnn_w2, L1_gnn_b2, L1_gnn_gamma, L1_gnn_beta):
    import jax
    import jax.numpy as jnp

    def _L0_gnn_ref(x, edge_index, W1, b1, W2, b2, W3, b3):
        import jax, jax.numpy as jnp
        import numpy as np
        N_NODES = 6250
        N_EDGES = 100000
        D_IN = 128
        U = 128
        H = 128
        h = x @ W1 + b1
        src = edge_index[0]
        dst = edge_index[1]
        h_i = h[dst]
        h_j = h[src]
        e = jnp.concatenate([h_i, h_j - h_i], axis=-1)
        m = jax.nn.relu(e @ W2 + b2)
        m = jax.nn.relu(m @ W3 + b3)
        out = jax.ops.segment_max(m, dst, num_segments=N_NODES)
        return jax.nn.relu(out)

    def _L1_gnn_ref(node_feats, src, dst, we_dst, we_src, be, w_proj, b_proj, w1, b1, w2, b2, gamma, beta):
        import jax, jax.numpy as jnp
        import numpy as np
        N = 6250
        E = 200000
        D = 128
        G = 128
        EPS = 1e-05
        NEG_SLOPE = 0.01
        ld = node_feats @ we_dst
        ls = node_feats @ we_src
        logit = ld[dst] + ls[src] + be
        logit = jnp.where(logit >= 0, logit, NEG_SLOPE * logit)
        m = jax.ops.segment_max(logit, dst, num_segments=N)
        ev = jnp.exp(logit - m[dst])
        denom = jax.ops.segment_sum(ev, dst, num_segments=N)
        a = ev / denom[dst]
        hv = node_feats @ w_proj + b_proj
        msg = hv[src] * a[:, None]
        c = jax.ops.segment_sum(msg, dst, num_segments=N)
        context = jax.nn.elu(c)
        h = jnp.concatenate([context, node_feats], axis=1)
        h = jax.nn.relu(h @ w1 + b1)
        h = h @ w2 + b2
        h = jax.nn.relu(h)
        mean = jnp.mean(h, axis=0)
        var = jnp.mean((h - mean) ** 2, axis=0)
        return gamma * (h - mean) / jnp.sqrt(var + EPS) + beta
    edge_index = jnp.stack([src, dst])
    x = _layernorm(x + _L0_gnn_ref(x, edge_index, L0_gnn_W1, L0_gnn_b1, L0_gnn_W2, L0_gnn_b2, L0_gnn_W3, L0_gnn_b3), axis=-1)
    x = _layernorm(x + _L1_gnn_ref(x, src, dst, L1_gnn_we_dst, L1_gnn_we_src, L1_gnn_be, L1_gnn_w_proj, L1_gnn_b_proj, L1_gnn_w1, L1_gnn_b1, L1_gnn_w2, L1_gnn_b2, L1_gnn_gamma, L1_gnn_beta), axis=-1)
    return x

_drawn_inputs = setup_inputs


def setup_inputs(seed=0):
    import zlib

    import numpy as np

    out = dict(_drawn_inputs(seed))
    spreads = {'L1_gnn_b_proj': (0.0, 0.1),
     'L1_gnn_b1': (0.0, 0.1),
     'L1_gnn_b2': (0.0, 0.1),
     'L1_gnn_gamma': (1.0, 0.2),
     'L1_gnn_beta': (0.0, 0.1)}
    factors = {'L0_gnn_b1': 8.0, 'L0_gnn_b2': 7.03, 'L0_gnn_b3': 5.819, 'L1_gnn_we_dst': 3.024}
    for name, (base, spread) in spreads.items():
        noise = np.random.default_rng([zlib.crc32(name.encode()), seed]).standard_normal(out[name].shape)
        drawn = base * np.exp(spread * noise) if base else spread * noise
        out[name] = jnp.asarray(drawn.astype(out[name].dtype))
    for name, factor in factors.items():
        out[name] = (out[name] * factor).astype(out[name].dtype)
    return out
```

```python
import concourse.bass as bass
from concourse import mybir
from contextlib import ExitStack

N = 6250
E = 206250
F = 128
T = 128
TILES = -(-E // T)
PASS = 52
PASSES = TILES // PASS
GT = 4
GROUPS = PASS // GT
SC = PASS // 2
ROWS = 124
COLS = TILES // ROWS
HALVES = 25
BLOCKS = 2 * HALVES
NP = BLOCKS * 128
LAST = N - (BLOCKS - 2) * 128
TAB = 132
CH = 512
CHUNKS = N // CH
EPS = 1e-5
SLOPE = 0.01
NEG = -1.0e38
assert TILES == PASS * PASSES == ROWS * COLS and PASS == GT * GROUPS


def build(nc, x, src, dst, W1, b1, W2, b2, W3, b3, we_dst, we_src, be, w_proj, b_proj,
          w1, bb1, w2, bb2, gamma, beta, out):
    fp32, bf16, i32 = mybir.dt.float32, mybir.dt.bfloat16, mybir.dt.int32
    ALU, ACT = mybir.AluOpType, mybir.ActivationFunctionType
    ds = bass.ds
    nc.disable_value_cache = True

    p_tab = nc.dram_tensor("p_tab", (NP, F), fp32, kind="Internal").ap()
    q_tab = nc.dram_tensor("q_tab", (NP, F), fp32, kind="Internal").ap()
    x1_tab = nc.dram_tensor("x1_tab", (NP, TAB), fp32, kind="Internal").ap()
    meta = nc.dram_tensor("meta", (4, TILES * T), bf16, kind="Internal").ap()
    cont_d = nc.dram_tensor("cont_d", (1, TILES), fp32, kind="Internal").ap()

    ctx = ExitStack()
    with ctx:
        def sb(name, shape, dt=fp32):
            return ctx.enter_context(nc.sbuf_tensor(name, shape, dt))

        def sem(name):
            return ctx.enter_context(nc.semaphore(name))

        ident, iota_n, ones = sb("ident", [128, 128]), sb("iota_n", [128, 128]), sb("ones", [128, 128])
        iota_p = sb("iota_p", [128, 1])
        W1s, W2s, Wpq, W3s = sb("W1s", [128, 128]), sb("W2s", [128, 2, 128]), sb("Wpq", [128, 2, 128]), sb("W3s", [128, 128])
        wprojs, w1s, w2s = sb("wprojs", [128, 128]), sb("w1s", [128, 2, 128]), sb("w2s", [128, 128])
        brow = sb("brow", [128, 2, 128])
        wsrc_row = sb("wsrc_row", [128, 128])
        cols = sb("cols", [128, 9])
        B1, B3, BP, BB1, BB2, GAM, BET, WDST, BE = (cols[:, i:i + 1] for i in range(9))
        srcT, relT, endT = sb("srcT", [128, TILES], i32), sb("relT", [128, TILES]), sb("endT", [128, TILES])
        rows = sb("rows", [128, TILES])
        cont = rows[0:1, :]
        base = rows[64:65, :].bitcast(i32)
        idx = sb("idx", [128, PASS], i32)
        X = sb("X", [128, BLOCKS, TAB])
        accT = sb("accT", [128, NP])
        G = sb("G", [128, PASS, TAB])
        ZW = 20992
        Z = sb("Z", [128, ZW])
        stats = sb("stats", [128, BLOCKS, 6])
        mean, var, rstd, nmr, tmp = (sb(n, [128, BLOCKS]) for n in ("mean", "var", "rstd", "nmr", "tmp"))
        bnst, bnmv = sb("bnst", [128, CHUNKS + 1, 6]), sb("bnmv", [128, 2])
        scl, shf, eps = sb("scl", [128, 1]), sb("shf", [128, 1]), sb("eps", [128, 1])

        top = [0]

        def z(shape, dt=fp32):
            n = 1
            for s in shape:
                n *= s
            words = n if dt != bf16 else n // 2
            assert top[0] + words <= ZW
            part = Z[:, top[0]:top[0] + words]
            top[0] += words
            assert top[0] <= ZW, top[0]
            if dt != fp32:
                part = part.bitcast(dt)
            if len(shape) == 2:
                part = part.rearrange("p (a b) -> p a b", a=shape[0])
            if len(shape) == 3:
                part = part.rearrange("p (a b c) -> p a b c", a=shape[0], b=shape[1])
            return part

        D = z([COLS, T + 2], i32)
        S0 = z([COLS, T], i32)
        srcF, rel, relend, flag = z([COLS, T]), z([COLS, T]), z([COLS, T]), z([COLS, T])
        metaS = z([4, COLS, T], bf16)
        contS = z([COLS])
        xin = [z([2, 128]) for _ in range(2)]
        xTs = [z([256]) for _ in range(2)]
        hTs = [z([256]) for _ in range(2)]
        pqs = [z([2, 256]) for _ in range(2)]
        top[0] = 0
        Pwin = z([PASS, 128])
        bc = z([2, PASS * T], bf16)
        OH = [z([CH]) for _ in range(3)]
        M1 = [z([CH]) for _ in range(3)]
        S = [z([CH]) for _ in range(3)]
        STs = [z([CH]) for _ in range(3)]
        EOH = [z([GT, 128]) for _ in range(3)]
        top[0] = 0
        cacc = z([2, NP])
        H = cacc[:, 0, :]
        ldbc = z([NP])
        z2 = top[0]
        top[0] = z2 - NP
        rec, Y, mn, mx, ex, ctxb, h1 = ([z([CH]) for _ in range(2)] for _ in range(7))
        outs = [z([2, 128]) for _ in range(2)]
        stg = [sb(f"stg{i}", [128, 256]) for i in range(2)]
        mt = sb("mt", [128, 2, 3, T], bf16)
        ldE, zE, lgE = sb("ldE", [128, 2, SC]), sb("zE", [128, SC]), sb("lgE", [128, SC])
        fw, bk, mM = sb("fw", [128, T]), sb("bk", [128, T]), sb("mM", [128, T])
        run = sb("run", [128, 2, SC + 1])
        carry = sb("carry", [128, 1])
        dif, exd = sb("dif", [128, T + 1]), sb("exd", [128, T + 1])
        evr = sb("evr", [128, 2, 2, SC])
        A = sb("A", [128, 4, 128])
        junk = sb("junk", [128, 4, 128], bf16)
        cr = sem("cr")

        bank = [ctx.enter_context(nc.psum_tensor(f"bank{i}", [128, 512], fp32)) for i in range(8)]

        weights_in, x_in, lists_in, base_in, rows_in = (sem(n) for n in ("weights_in", "x_in", "lists_in", "base_in", "rows_in"))
        consts, pads, prep = sem("consts"), sem("pads"), sem("prep")
        xin_in = [sem(f"xin_in{i}") for i in range(2)]
        xt_tr, xt_cp, h_mm, h_ev, pq_mm, pq_ev = (sem(n) for n in ("xt_tr", "xt_cp", "h_mm", "h_ev", "pq_mm", "pq_ev"))
        pq_out = [sem(f"pq_out{i}") for i in range(2)]
        meta_out, cont_out, list_tr, list_ev = sem("meta_out"), sem("cont_out"), sem("list_tr"), sem("list_ev")
        idx_ok = sem("idx_ok")
        landed = [sem(f"landed{g}") for g in range(GROUPS)]
        win_in = [sem(f"win_in{g}") for g in range(GROUPS)]
        bc_in = [sem(f"bc_in{i}") for i in range(2)]
        oh_ok, x_mm, relu_ok, v_mm, scan_ok, s_tr, st_ok, eoh_ok, o_mm, acc_ok = (sem(n) for n in (
            "oh_ok", "x_mm", "relu_ok", "v_mm", "scan_ok", "s_tr", "st_ok", "eoh_ok", "o_mm", "acc_ok"))
        n1_st, n1_tr, n1_add, n1_bn, stat_ok, sq_ok = (sem(n) for n in ("n1_st", "n1_tr", "n1_add", "n1_bn", "stat_ok", "sq_ok"))
        nm_ok, ls_ok, cp_ok, n1_t2, x1t_ok, ld_mm, ldb_ok, tab_out = (sem(n) for n in (
            "nm_ok", "ls_ok", "cp_ok", "n1_t2", "x1t_ok", "ld_mm", "ldb_ok", "tab_out"))
        cleared = sem("cleared")
        meta_in = [sem(f"meta_in{i}") for i in range(2)]
        rows_landed = [sem(f"rows_landed{i}") for i in range(2)]
        ld_ok, lg_ok, lg_tr, sc_ok, last_tr, run_ok, run_tr, dif_ok, exp_ok, ev_tr, ev_ok = (sem(n) for n in (
            "ld_ok", "lg_ok", "lg_tr", "sc_ok", "last_tr", "run_ok", "run_tr", "dif_ok", "exp_ok", "ev_tr", "ev_ok"))
        a_ok, t_mm, sum_ok = sem("a_ok"), sem("t_mm"), sem("sum_ok")
        y_ok, c_mm, mm_ok, ex_ok, ctx_ok, h1_mm, h1_ok, h2_mm, h2_ok, bn_ok = (sem(n) for n in (
            "y_ok", "c_mm", "mm_ok", "ex_ok", "ctx_ok", "h1_mm", "h1_ok", "h2_mm", "h2_ok", "bn_ok"))
        aff_ok, n2_st, n2_tr, n2_add, n2_bn, stat2_ok, sq2_ok, nm2_ok = (sem(n) for n in (
            "aff_ok", "n2_st", "n2_tr", "n2_add", "n2_bn", "stat2_ok", "sq2_ok", "nm2_ok"))
        out_done = [sem(f"out_done{i}") for i in range(2)]
        turns = {e: sem(f"turns_{e}") for e in ("pool", "act", "dve", "pe", "sp")}

        def after(eng, s, n):
            if not isinstance(n, int) or n > 0:
                eng.wait_ge(s, n)

        def settle(eng, name):
            eng.sem_inc(turns[name], 1)

        def over(eng, full, stages, width=None, tail=None):
            lag = max(k for k, _ in stages)
            first = 4

            def step(h, p, static):
                for k, f in stages:
                    if static and not 0 <= h - k <= full:
                        continue
                    f(h - k, (p - k) % 2, tail if static and h - k == full else width)

            for h in range(first):
                step(h, h % 2, True)
            assert lag <= first and full % 2 == 0
            with eng.Fori(first // 2, full // 2) as i:
                step(i * 2, 0, False)
                step(i * 2 + 1, 1, False)
            for h in range(full, full + 1 + lag):
                step(h, h % 2, True)

        def groups(eng, stages):
            def a_pass(i, upto=GROUPS):
                for g in range(upto):
                    for k, f in stages:
                        gg, ii = (g - k, i) if g >= k else (g - k + GROUPS, i - 1)
                        if isinstance(i, int) and (ii < 0 or ii >= PASSES):
                            continue
                        f(ii * GROUPS + gg, gg, ii)

            a_pass(0)
            with eng.Fori(1, PASSES) as i:
                a_pass(i)
            a_pass(PASSES, max(k for k, _ in stages))

        def used2(k, g):
            return k if g == 0 else k - 1

        def ring(g):
            return 2 if g == GROUPS - 1 else g % 2

        block = ctx.enter_context(nc.Block())

        @block.sync
        def _(sp):
            for to, of in ((W1s[:, :], W1[:, :]), (W2s[:, :, :], W2.rearrange("(a k) n -> k a n", a=2)),
                           (W3s[:, :], W3[:, :]), (wprojs[:, :], w_proj[:, :]),
                           (w1s[:, :, :], w1.rearrange("(a k) n -> k a n", a=2)), (w2s[:, :], w2[:, :]),
                           (brow[:, 0, :], b2.rearrange("(a n) -> a n", a=1).broadcast_to([128, 128])),
                           (wsrc_row[:, :], we_src.rearrange("(a n) -> a n", a=1).broadcast_to([128, 128]))):
                sp.dma_start(to, of).then_inc(weights_in, 16)
            with nc.allow_non_contiguous_dma(reason="a few vectors"):
                for to, of in ((B1, b1), (B3, b3), (BP, b_proj), (BB1, bb1), (BB2, bb2), (GAM, gamma),
                               (BET, beta), (WDST, we_dst)):
                    sp.dma_start(to, of.rearrange("(n a) -> n a", a=1)).then_inc(weights_in, 16)
                sp.dma_start(BE, be.rearrange("(n a) -> n a", a=1).broadcast_to([128, 1])).then_inc(weights_in, 16)
                sp.dma_start(base[:, 0:TILES - 1], dst[0:(TILES - 1) * T].rearrange("(t e) -> e t", e=T)[0:1, :]).then_inc(base_in, 16)
                sp.dma_start(base[:, TILES - 1:TILES], dst[(TILES - 1) * T:(TILES - 1) * T + 1].rearrange("(a n) -> a n", a=1)).then_inc(base_in, 16)
            sp.wait_ge(pads, 4)
            sp.dma_start(X[:, 0:BLOCKS - 2, 0:F], x[0:(BLOCKS - 2) * 128, :].rearrange("(b p) f -> p b f", p=128)).then_inc(x_in, 16)
            sp.dma_start(X[0:LAST, BLOCKS - 2, 0:F], x[(BLOCKS - 2) * 128:N, :]).then_inc(x_in, 16)

            def load_x(h, p, w):
                after(sp, xt_tr, h - 1)
                settle(sp, "sp")
                if w:
                    sp.dma_start(xin[p][0:LAST, 0, :], x[(BLOCKS - 2) * 128:N, :]).then_inc(xin_in[p], 16)
                else:
                    sp.dma_start(xin[p], x[ds(h * 256, 256), :].rearrange("(b p) f -> p b f", p=128)).then_inc(xin_in[p], 16)

            def store_pq(h, p, w):
                sp.wait_ge(pq_ev, h + 1)
                settle(sp, "sp")
                for tab, o in ((p_tab, 0), (q_tab, 128)):
                    sp.dma_start(tab[ds(h * 256, 256), :].rearrange("(b p) f -> p b f", p=128),
                                 pqs[p][:, :, o:o + 128]).then_inc(pq_out[p], 16)

            over(sp, HALVES - 1, [(0, load_x), (3, store_pq)], tail=1)

            sp.wait_ge(prep, 7)
            for k in range(4):
                sp.dma_start(meta[k, :].rearrange("(c p e) -> p c e", p=ROWS, e=T), metaS[0:ROWS, k]).then_inc(meta_out, 16)
            with nc.allow_non_contiguous_dma(reason="one number for each tile"):
                sp.dma_start(cont_d[0, :].rearrange("(c p) -> p c", p=ROWS), contS[0:ROWS, :]).then_inc(cont_out, 16)
            sp.wait_ge(cont_out, 16)
            sp.dma_start(cont, cont_d[:, :]).then_inc(rows_in, 16)
            sp.wait_ge(meta_out, 64)
            sp.wait_ge(base_in, 32)
            sp.wait_ge(pq_out[0], 32 * 13)
            sp.wait_ge(pq_out[1], 32 * 12)
            sp.wait_ge(cont_out, 16)
            sp.wait_ge(list_tr, 3 * COLS)

            def windows(i, g):
                at = [sp.value_load(base[0:1, ds(i * PASS + g * GT + j, 1)], min_val=0, max_val=NP - 128) for j in range(GT)]
                after(sp, x_mm, (i - 1) * GROUPS + g + 1)
                settle(sp, "sp")
                for j in range(GT):
                    sp.dma_start(Pwin[:, g * GT + j, :], p_tab[ds(at[j], 128), :]).then_inc(win_in[g], 16)

            def spread(i, half):
                a, b = ((0, 7), (7, GROUPS))[half]
                after(sp, scan_ok, (i - 1) * GROUPS + b)
                after(sp, oh_ok, (i - 1) * GROUPS + b)
                settle(sp, "sp")
                for k in range(2):
                    sp.dma_start(bc[:, k, a * CH:b * CH],
                                 meta[k:k + 1, ds(i * (PASS * T) + a * CH, (b - a) * CH)].broadcast_to([128, (b - a) * CH])).then_inc(bc_in[half], 16)

            def first_layer(i):
                spread(i, 0)
                for g in range(7):
                    windows(i, g)
                spread(i, 1)
                for g in range(7, GROUPS):
                    windows(i, g)

            first_layer(0)
            with sp.Fori(1, PASSES) as i:
                first_layer(i)

            def store_tab(h, p, w):
                sp.wait_ge(cp_ok, h + 1)
                sp.wait_ge(ls_ok, 2 * h + 2)
                settle(sp, "sp")
                sp.dma_start(x1_tab[ds(h * 256, 256), :].rearrange("(b p) f -> p b f", p=128), X[:, ds(h * 2, 2), :]).then_inc(tab_out, 16)

            over(sp, HALVES - 1, [(0, store_tab)])

            def load_masks(i, s):
                q = i * 2 + s
                after(sp, dif_ok, q - 1)
                settle(sp, "sp")
                sp.dma_start(mt[0:SC, s], meta[1:4, ds(q * (SC * T), SC * T)].rearrange("k (t e) -> t k e", e=T)).then_inc(meta_in[s], 16)

            for s in range(2):
                load_masks(0, s)
            with sp.Fori(1, PASSES) as i:
                for s in range(2):
                    load_masks(i, s)

            def store_out(h, p, w):
                sp.wait_ge(nm2_ok, 2 * h + 2)
                settle(sp, "sp")
                if w:
                    sp.dma_start(out[(BLOCKS - 2) * 128:N, :], outs[p][0:LAST, 0, :]).then_inc(out_done[p], 16)
                else:
                    sp.dma_start(out[ds(h * 256, 256), :].rearrange("(b p) f -> p b f", p=128), outs[p]).then_inc(out_done[p], 16)

            over(sp, HALVES - 1, [(0, store_out)], tail=1)
            sp.wait_ge(out_done[0], 16 * 13)
            sp.wait_ge(out_done[1], 16 * 12)

        @block.gpsimd
        def _(pool):
            nc.gpsimd.memset(ident[:, :], 0.0).then_inc(turns["pool"], 1)
            nc.gpsimd.memset(D[:, :, :], -1).then_inc(pads, 1)
            nc.gpsimd.memset(S0[:, :, :], 0).then_inc(pads, 1)
            nc.gpsimd.memset(X[:, BLOCKS - 2:BLOCKS, :], 0.0).then_inc(pads, 1)
            nc.gpsimd.memset(X[:, 0:BLOCKS - 2, F:TAB], 0.0).then_inc(pads, 1)
            nc.gpsimd.iota(iota_n[:, :], pattern=[[1, 128]], base=0, channel_multiplier=0, allow_small_or_imprecise_dtypes=True).then_inc(consts, 1)
            nc.gpsimd.iota(iota_p[:, :], pattern=[[0, 1]], base=0, channel_multiplier=1, allow_small_or_imprecise_dtypes=True).then_inc(consts, 1)
            nc.gpsimd.memset(ones[:, :], 1.0).then_inc(consts, 1)
            nc.gpsimd.memset(eps[:, :], EPS).then_inc(consts, 1)
            nc.gpsimd.memset(run[:, :, :], NEG).then_inc(consts, 1)
            nc.gpsimd.memset(brow[:, 1, :], 0.0).then_inc(consts, 1)
            pool.wait_ge(turns["pool"], 1)
            nc.gpsimd.affine_select(out=ident[:, :], in_=ident[:, :], compare_op=ALU.not_equal, fill=1.0, base=0,
                                    pattern=[[-1, 128]], channel_multiplier=1).then_inc(consts, 1)
            pool.wait_ge(pads, 2)
            whole = ROWS * T
            end = (COLS - 1) * whole
            pool.dma_start(D[0:1, 0, 1:T + 2], dst[0:T + 1].rearrange("(a n) -> a n", a=1)).then_inc(lists_in, 16)
            pool.dma_start(D[1:ROWS, 0, 0:T + 2], bass.AP(dst.tensor, T - 1, [[T, ROWS - 1], [1, T + 2]])).then_inc(lists_in, 16)
            pool.dma_start(D[0:ROWS, 1:COLS - 1, 0:T + 2], bass.AP(dst.tensor, whole - 1, [[T, ROWS], [whole, COLS - 2], [1, T + 2]])).then_inc(lists_in, 16)
            pool.dma_start(D[0:ROWS - 1, COLS - 1, 0:T + 2], bass.AP(dst.tensor, end - 1, [[T, ROWS - 1], [1, T + 2]])).then_inc(lists_in, 16)
            pool.dma_start(D[ROWS - 1:ROWS, COLS - 1, 0:E - (TILES - 1) * T + 1], dst[(TILES - 1) * T - 1:E].rearrange("(a n) -> a n", a=1)).then_inc(lists_in, 16)
            pool.dma_start(S0[0:ROWS, 0:COLS - 1, :], src[0:end].rearrange("(c p e) -> p c e", p=ROWS, e=T)).then_inc(lists_in, 16)
            pool.dma_start(S0[0:ROWS - 1, COLS - 1, :], src[end:(TILES - 1) * T].rearrange("(p e) -> p e", e=T)).then_inc(lists_in, 16)
            pool.dma_start(S0[ROWS - 1:ROWS, COLS - 1, 0:E - (TILES - 1) * T], src[(TILES - 1) * T:E].rearrange("(a n) -> a n", a=1)).then_inc(lists_in, 16)
            nc.gpsimd.memset(accT[:, :], 0.0).then_inc(cleared, 1)

            half = PASS // 2

            def indices(i, s, free):
                for f, n in free:
                    after(pool, f, n)
                settle(pool, "pool")
                nc.gpsimd.tensor_copy(idx[:, s * half:(s + 1) * half], srcT[:, ds(i * PASS + s * half, half)]).then_inc(idx_ok, 1)

            pool.wait_ge(list_ev, 12)
            pool.wait_ge(pq_out[0], 32 * 13)
            pool.wait_ge(pq_out[1], 32 * 12)

            def gather_q(i):
                indices(i, 0, [(landed[g], i * 64) for g in range(7)])
                pool.wait_ge(idx_ok, i * 2 + 1)
                for g in range(GROUPS):
                    if g == 6:
                        indices(i, 1, [(landed[u], i * 64) for u in range(7, GROUPS)] + [(landed[6], i * 64)])
                        pool.wait_ge(idx_ok, i * 2 + 2)
                    after(pool, x_mm, (i - 1) * GROUPS + g + 1)
                    settle(pool, "pool")
                    for j in range(g * GT, g * GT + GT):
                        pool.indirect_dma_start(G[:, j, 0:F], None, q_tab[:, :],
                                                bass.IndirectOffsetOnAxis(ap=idx[:, j:j + 1], axis=0)).then_inc(landed[g], 16)

            gather_q(0)
            with pool.Fori(1, PASSES) as i:
                gather_q(i)

            pool.wait_ge(acc_ok, TILES)
            nc.gpsimd.memset(cacc, 0.0).then_inc(cleared, 1)
            for g in range(GROUPS):
                pool.wait_ge(landed[g], 64 * PASSES)
            pool.wait_ge(tab_out, 16 * HALVES)

            def gather_x1(i):
                for s in range(2):
                    indices(i, s, [(rows_landed[s], i * (16 * SC))])
                    pool.wait_ge(idx_ok, (i + PASSES) * 2 + s + 1)
                    for j in range(SC):
                        if j % 13 == 0:
                            after(pool, t_mm, (i - 1) * PASS + s * SC + j + 13)
                            after(pool, lg_ok, 2 * (i * 2 + s - 1))
                            settle(pool, "pool")
                        u = s * SC + j
                        pool.indirect_dma_start(G[:, u, :], None, x1_tab[:, :],
                                                bass.IndirectOffsetOnAxis(ap=idx[:, u:u + 1], axis=0)).then_inc(rows_landed[s], 16)

            gather_x1(0)
            with pool.Fori(1, PASSES) as i:
                gather_x1(i)

        @block.scalar
        def _(act):
            act.wait_ge(weights_in, 16 * 17)
            act.wait_ge(consts, 7)

            def h_evac(h, p, w):
                act.wait_ge(h_mm, h + 1)
                after(act, pq_mm, h - 1)
                nc.scalar.activation(hTs[p], bank[2 + p][:, 0:256], ACT.Identity, bias=B1).then_inc(h_ev, 1)

            over(act, HALVES - 1, [(0, h_evac)])
            for k, (to, n) in enumerate(((srcT, 0), (relT, 1), (endT, 2))):
                for c in range(0, COLS, 4):
                    w = min(4, COLS - c)
                    act.wait_ge(list_tr, n * COLS + c + w)
                    nc.scalar.copy(to[:, c * ROWS:(c + w) * ROWS], bank[6 + (n * 4 + c // 4) % 2][:, 0:w * ROWS]).then_inc(list_ev, 1)

            def relu(k, g, i):
                act.wait_ge(x_mm, k + 1)
                after(act, v_mm, k - 1)
                nc.scalar.activation(M1[ring(g)], bank[g % 2][:, :], ACT.Relu).then_inc(relu_ok, 1)

            def evac(k, g, i):
                act.wait_ge(s_tr, k + 1)
                after(act, o_mm, k - 1)
                nc.scalar.copy(STs[ring(g)], bank[4 + g % 2][:, :]).then_inc(st_ok, 1)

            groups(act, [(0, relu), (3, evac)])

            act.wait_ge(acc_ok, TILES)

            def bias_relu(h, p, w):
                after(act, n1_tr, h - 1)
                settle(act, "act")
                nc.scalar.activation(stg[p][:, :], accT[:, ds(h * 256, 256)], ACT.Relu, bias=B3).then_inc(n1_st, 1)

            over(act, HALVES - 1, [(0, bias_relu)])
            act.wait_ge(stat_ok, 1)
            nc.scalar.activation(tmp[:, :], var[:, :], ACT.Sqrt, bias=eps[:, :]).then_inc(sq_ok, 1)

            def keep(h, p, w):
                act.wait_ge(nm_ok, 2 * h + 2)
                settle(act, "act")
                nc.scalar.copy(X[:, ds(h * 2, 2), 0:F], stg[p][:, :].rearrange("p (b f) -> p b f", b=2)).then_inc(cp_ok, 1)

            def keep_t(h, p, w):
                act.wait_ge(n1_t2, h + 1)
                settle(act, "act")
                nc.scalar.copy(accT[:, ds(h * 256, 256)], bank[2 + p][:, 0:256]).then_inc(x1t_ok, 1)

            def keep_ld(h, p, w):
                act.wait_ge(ld_mm, h + 1)
                settle(act, "act")
                nc.scalar.activation(ldbc[:, ds(h * 256, 256)], bank[4 + p][:, 0:256], ACT.Identity, bias=BE).then_inc(ldb_ok, 1)

            over(act, HALVES - 1, [(0, keep), (0, keep_t), (1, keep_ld)])

            def weights(i, s):
                q = i * 2 + s
                act.wait_ge(dif_ok, q + 1)
                after(act, ev_tr, q)
                nc.scalar.activation(exd[0:SC, :], dif[0:SC, :], ACT.Exp).then_inc(exp_ok, 1)
                act.wait_ge(ev_tr, q + 1)
                after(act, sum_ok, (q - 1) * SC)
                nc.scalar.copy(evr[:, s], bank[7][:, 0:2 * SC].rearrange("p (a t) -> p a t", a=2)).then_inc(ev_ok, 1)

            for s in range(2):
                weights(0, s)
            with act.Fori(1, PASSES) as i:
                for s in range(2):
                    weights(i, s)

            def expo(c, p, w):
                act.wait_ge(mm_ok, c + 1)
                after(act, ctx_ok, c - 1)
                nc.scalar.activation(ex[p][:, 0:w], mn[p][:, 0:w], ACT.Exp).then_inc(ex_ok, 1)

            def relu1(c, p, w):
                act.wait_ge(h1_mm, c + 1)
                after(act, h2_mm, c - 1)
                nc.scalar.activation(h1[p][:, 0:w], bank[2 + p][:, 0:w], ACT.Relu, bias=BB1).then_inc(h1_ok, 1)

            def relu2(c, p, w):
                act.wait_ge(h2_mm, c + 1)
                settle(act, "act")
                nc.scalar.activation(H[:, ds(c * CH, w)], bank[4 + p][:, 0:w], ACT.Relu, bias=BB2).then_inc(h2_ok, 1)

            over(act, CHUNKS, [(0, expo), (1, relu1), (2, relu2)], width=CH, tail=N - CHUNKS * CH)
            act.wait_ge(aff_ok, 2)
            nc.scalar.activation(scl[:, :], bnmv[:, 1:2], ACT.Sqrt, bias=eps[:, :]).then_inc(aff_ok, 1)
            act.wait_ge(aff_ok, 7)

            def affine(h, p, w):
                after(act, n2_tr, h - 1)
                settle(act, "act")
                nc.scalar.activation(stg[p][:, :], H[:, ds(h * 256, 256)], ACT.Identity, bias=shf[:, :], scale=scl[:, :]).then_inc(n2_st, 1)

            over(act, HALVES - 1, [(0, affine)])
            act.wait_ge(stat2_ok, 1)
            nc.scalar.activation(tmp[:, :], var[:, :], ACT.Sqrt, bias=eps[:, :]).then_inc(sq2_ok, 1)

        @block.tensor
        def _(pe):
            pe.wait_ge(weights_in, 16 * 17)
            pe.wait_ge(consts, 7)

            def tr_x(h, p, w):
                pe.wait_ge(xin_in[p], (h - p) * 8 + 16)
                after(pe, xt_cp, h - 1)
                for b in range(2):
                    last = nc.tensor.transpose(bank[p][:, b * 128:(b + 1) * 128], xin[p][:, b, :], ident[:, :])
                last.then_inc(xt_tr, 1)

            def mm_h(h, p, w):
                pe.wait_ge(xt_cp, h + 1)
                after(pe, h_ev, h - 1)
                nc.tensor.matmul(bank[2 + p][:, 0:256], W1s[:, :], xTs[p], start=True, stop=True).then_inc(h_mm, 1)

            def mm_pq(h, p, w):
                pe.wait_ge(h_ev, h + 1)
                after(pe, pq_ev, h - 1)
                for b in range(2):
                    last = nc.tensor.matmul(bank[4 + p][:, b * 256:(b + 1) * 256], hTs[p][:, b * 128:(b + 1) * 128],
                                            Wpq[:, :, :].rearrange("k a n -> k (a n)"), start=True, stop=True)
                last.then_inc(pq_mm, 1)

            pe.wait_ge(prep, 1)
            over(pe, HALVES - 1, [(0, tr_x), (1, mm_h), (2, mm_pq)])
            for n, (of, need) in enumerate(((srcF, 2), (rel, 3), (relend, 6))):
                pe.wait_ge(prep, need)
                for c in range(COLS):
                    u = n * 4 + c // 4
                    if c % 4 == 0:
                        after(pe, list_ev, u - 1)
                    nc.tensor.transpose(bank[6 + u % 2][:, c % 4 * ROWS:(c % 4 + 1) * ROWS], of[0:ROWS, c, :],
                                        ident[0:ROWS, 0:ROWS]).then_inc(list_tr, 1)

            def pre(k, g, i):
                pe.wait_ge(landed[g], i * 64 + 64)
                pe.wait_ge(win_in[g], i * 64 + 64)
                pe.wait_ge(oh_ok, k + 1)
                after(pe, relu_ok, used2(k, g))
                for j in range(GT):
                    o = bank[g % 2][:, j * 128:(j + 1) * 128]
                    nc.tensor.matmul(o, G[:, g * GT + j, 0:F], ident[:, :], start=True, stop=False)
                    last = nc.tensor.matmul(o, Pwin[:, g * GT + j, :], OH[ring(g)][:, j * 128:(j + 1) * 128], start=False, stop=True)
                last.then_inc(x_mm, 1)

            def mm3(k, g, i):
                pe.wait_ge(relu_ok, k + 1)
                after(pe, scan_ok, used2(k, g))
                nc.tensor.matmul(bank[2 + g % 2][:, :], W3s[:, :], M1[ring(g)], start=True, stop=True).then_inc(v_mm, 1)

            def tr_s(k, g, i):
                pe.wait_ge(scan_ok, k + 1)
                after(pe, st_ok, used2(k, g))
                for j in range(GT):
                    last = nc.tensor.transpose(bank[4 + g % 2][:, j * 128:(j + 1) * 128], S[ring(g)][:, j * 128:(j + 1) * 128], ident[:, :])
                last.then_inc(s_tr, 1)

            def pick(k, g, i):
                pe.wait_ge(st_ok, k + 1)
                pe.wait_ge(eoh_ok, k + 1)
                after(pe, acc_ok, used2(k, g) * GT)
                for j in range(GT):
                    last = nc.tensor.matmul(bank[6 + g % 2][:, j * 128:(j + 1) * 128], STs[ring(g)][:, j * 128:(j + 1) * 128],
                                            EOH[ring(g)][:, j, :], start=True, stop=True)
                last.then_inc(o_mm, 1)

            groups(pe, [(0, pre), (1, mm3), (3, tr_s), (4, pick)])

            def tr_1(h, p, w):
                pe.wait_ge(n1_st, h + 1)
                after(pe, n1_add, h - 1)
                for b in range(2):
                    last = nc.tensor.transpose(bank[p][:, b * 128:(b + 1) * 128], stg[p][:, b * 128:(b + 1) * 128], ident[:, :])
                last.then_inc(n1_tr, 1)

            over(pe, HALVES - 1, [(0, tr_1)])

            def tr_2(h, p, w):
                pe.wait_ge(nm_ok, 2 * h + 2)
                after(pe, x1t_ok, h - 1)
                for b in range(2):
                    last = nc.tensor.transpose(bank[2 + p][:, b * 128:(b + 1) * 128], stg[p][:, b * 128:(b + 1) * 128], ident[:, :])
                last.then_inc(n1_t2, 1)

            def mm_ld(h, p, w):
                pe.wait_ge(x1t_ok, h + 1)
                after(pe, ldb_ok, h - 1)
                nc.tensor.matmul(bank[4 + p][:, 0:256], WDST.broadcast_to([128, 128]), accT[:, ds(h * 256, 256)], start=True, stop=True).then_inc(ld_mm, 1)

            over(pe, HALVES - 1, [(0, tr_2), (1, mm_ld)])

            def softmax_tr(i, s):
                q = i * 2 + s
                pe.wait_ge(lg_ok, 2 * q + 2)
                after(pe, dif_ok, q)
                nc.tensor.transpose(bank[4][0:SC, 0:T], lgE[:, :], ident[:, :]).then_inc(lg_tr, 1)
                pe.wait_ge(sc_ok, 3 * q + 2)
                settle(pe, "pe")
                nc.tensor.matmul(bank[5][0:1, 0:SC], fw[0:SC, T - 1:T], ident[0:SC, 0:SC], start=True, stop=True).then_inc(last_tr, 1)
                pe.wait_ge(run_ok, 2 * q + 2)
                settle(pe, "pe")
                nc.tensor.matmul(bank[6][0:SC, 0:1], run[0:1, s, 0:SC], ones[0:1, 0:1], start=True, stop=True).then_inc(run_tr, 1)
                pe.wait_ge(exp_ok, q + 1)
                after(pe, ev_ok, q)
                settle(pe, "pe")
                nc.tensor.transpose(bank[7][:, 0:SC], exd[0:SC, 0:T], ident[0:SC, 0:SC])
                nc.tensor.matmul(bank[7][:, SC:2 * SC], exd[0:SC, T:T + 1].broadcast_to([SC, 128]), ident[0:SC, 0:SC],
                                 start=True, stop=True).then_inc(ev_tr, 1)

            def sums(i, s, j):
                t = i * PASS + s * SC + j
                u = (s * SC + j) % 4
                pe.wait_ge(a_ok, t + 1)
                after(pe, sum_ok, t - 3)
                nc.tensor.matmul(bank[u][:, 0:128], G[:, s * SC + j, 0:F], A[:, u, :], start=True, stop=True)
                nc.tensor.matmul(bank[u][:, 128:256], ones[:, :], A[:, u, :], start=True, stop=True).then_inc(t_mm, 1)

            def second(i):
                for s in range(2):
                    softmax_tr(i, s)
                    for j in range(SC):
                        sums(i, s, j)

            second(0)
            with pe.Fori(1, PASSES) as i:
                second(i)

            def mm_c(c, p, w):
                pe.wait_ge(y_ok, 2 * c + 2)
                after(pe, mm_ok, c - 1)
                nc.tensor.matmul(bank[p][:, 0:w], wprojs[:, :], Y[p][:, 0:w], start=True, stop=True).then_inc(c_mm, 1)

            def mm_h1(c, p, w):
                pe.wait_ge(ctx_ok, c + 1)
                after(pe, h1_ok, c - 1)
                nc.tensor.matmul(bank[2 + p][:, 0:w], w1s[:, 0, :], ctxb[p][:, 0:w], start=True, stop=False)
                nc.tensor.matmul(bank[2 + p][:, 0:w], w1s[:, 1, :], accT[:, ds(c * CH, w)], start=False, stop=True).then_inc(h1_mm, 1)

            def mm_h2(c, p, w):
                pe.wait_ge(h1_ok, c + 1)
                after(pe, h2_ok, c - 1)
                nc.tensor.matmul(bank[4 + p][:, 0:w], w2s[:, :], h1[p][:, 0:w], start=True, stop=True).then_inc(h2_mm, 1)

            over(pe, CHUNKS, [(0, mm_c), (1, mm_h1), (2, mm_h2)], width=CH, tail=N - CHUNKS * CH)

            def tr_3(h, p, w):
                pe.wait_ge(n2_st, h + 1)
                after(pe, n2_add, h - 1)
                for b in range(2):
                    last = nc.tensor.transpose(bank[p][:, b * 128:(b + 1) * 128], stg[p][:, b * 128:(b + 1) * 128], ident[:, :])
                last.then_inc(n2_tr, 1)

            over(pe, HALVES - 1, [(0, tr_3)])

        @block.vector
        def _(dve):
            v = nc.vector
            done = [0]

            def chain(ins):
                done[0] += 1
                ins.then_inc(turns["dve"], 1)
                dve.wait_ge(turns["dve"], done[0])

            dve.wait_ge(weights_in, 16 * 17)
            dve.wait_ge(consts, 7)
            v.tensor_copy(Wpq[:, 1, :], W2s[:, 1, :])
            v.tensor_tensor(Wpq[:, 0, :], W2s[:, 0, :], W2s[:, 1, :], ALU.subtract).then_inc(prep, 1)

            R = slice(0, ROWS)
            here, before, next_ = D[R, :, 1:T + 1], D[R, :, 0:T], D[R, :, 2:T + 2]
            dve.wait_ge(lists_in, 16 * 8)
            v.tensor_copy(srcF[R], S0[R]).then_inc(prep, 1)
            v.tensor_tensor(rel[R], here, D[R, :, 1:2].broadcast_to([ROWS, COLS, T]), ALU.subtract).then_inc(prep, 1)
            chain(v.tensor_tensor(flag[R], here, before, ALU.not_equal))
            dve.wait_ge(prep, 3)
            v.tensor_copy(metaS[R, 0], rel[R])
            v.tensor_scalar(metaS[R, 3], rel[R], 0.0, NEG, ALU.not_equal, ALU.mult)
            chain(v.tensor_scalar(metaS[R, 1], flag[R], NEG, None, ALU.mult))
            chain(v.tensor_scalar(contS[R, :], rel[R, :, T - 1:T].rearrange("p c e -> p (c e)"), 0.0, None, ALU.not_equal))
            v.scalar_tensor_tensor(out=contS[R, :], in0=contS[R, :], scalar=NEG, in1=metaS[R, 1, :, 0:1].rearrange("p c e -> p (c e)"),
                                   op0=ALU.mult, op1=ALU.add).then_inc(prep, 1)
            chain(v.tensor_tensor(flag[R], next_, here, ALU.not_equal))
            v.tensor_scalar(metaS[R, 2], flag[R], NEG, None, ALU.mult).then_inc(prep, 1)
            chain(v.scalar_tensor_tensor(out=relend[R], in0=rel[R], scalar=1.0, in1=flag[R], op0=ALU.add, op1=ALU.mult))
            chain(v.tensor_scalar(relend[R], relend[R], -1.0, None, ALU.add))
            v.engine_nop().then_inc(prep, 2)

            def cp_x(h, p, w):
                dve.wait_ge(xt_tr, h + 1)
                after(dve, h_mm, h - 1)
                v.tensor_copy(xTs[p], bank[p][:, 0:256]).then_inc(xt_cp, 1)

            def ev_pq(h, p, w):
                dve.wait_ge(pq_mm, h + 1)
                after(dve, pq_out[p], (h - p) * 16)
                v.tensor_tensor(pqs[p], bank[4 + p][:, :].rearrange("p (b n) -> p b n", b=2),
                                brow[:, :, :].rearrange("p a n -> p (a n)").unsqueeze(1).broadcast_to([128, 2, 256]), ALU.add).then_inc(pq_ev, 1)

            over(dve, HALVES - 1, [(0, cp_x), (2, ev_pq)])
            dve.wait_ge(list_ev, 12)
            dve.wait_ge(rows_in, 16)
            dve.wait_ge(base_in, 32)
            dve.wait_ge(cleared, 1)

            at = {}

            def one_hot(k, g, i):
                half = 0 if g < 7 else 1
                dve.wait_ge(bc_in[half], i * 32 + 32)
                after(dve, x_mm, k - 1)
                v.tensor_scalar(OH[ring(g)], bc[:, 0, g * CH:(g + 1) * CH], iota_p[:, :], None, ALU.is_equal).then_inc(oh_ok, 1)

            def scan(k, g, i):
                dve.wait_ge(v_mm, k + 1)
                after(dve, s_tr, k - 1)
                after(dve, scan_ok, k)
                first = isinstance(k, int) and k == 0
                v.tensor_tensor_scan(out=S[ring(g)], data0=bc[:, 1, g * CH:(g + 1) * CH], data1=bank[2 + g % 2][:, :],
                                     initial=NEG if first else S[ring((g - 1) % GROUPS)][:, CH - 1:CH], op0=ALU.add, op1=ALU.max).then_inc(scan_ok, 1)

            def ends(k, g, i):
                after(dve, o_mm, k - 1)
                v.tensor_tensor(EOH[ring(g)], iota_n[:, :].unsqueeze(1).broadcast_to([128, GT, 128]),
                                endT[:, ds(k * GT, GT)].unsqueeze(2).broadcast_to([128, GT, 128]), ALU.is_equal).then_inc(eoh_ok, 1)

            def add_up(j):
                def f(k, g, i):
                    at = dve.value_load(base[0:1, ds(k * GT + j, 1)], min_val=0, max_val=NP - 128)
                    win = accT[:, ds(at, 128)]
                    if j == 0:
                        dve.wait_ge(o_mm, k + 1)
                    after(dve, acc_ok, k * GT + j)
                    v.tensor_tensor(win, win, bank[6 + g % 2][:, j * 128:(j + 1) * 128], ALU.add).then_inc(acc_ok, 1)
                return f

            groups(dve, [(0, one_hot), (5, add_up(0)), (2, scan), (5, add_up(1)), (3, ends), (5, add_up(2)), (5, add_up(3))])

            def add_to_x(sem_tr, sem_add):
                def f(h, p, w):
                    dve.wait_ge(sem_tr, h + 1)
                    xs = X[:, ds(h * 2, 2), 0:F]
                    v.tensor_tensor(xs, xs, bank[p][:, 0:256].rearrange("p (b f) -> p b f", b=2), ALU.add).then_inc(sem_add, 1)
                return f

            def row_stats(sem_add, sem_bn):
                def f(h, p, w):
                    dve.wait_ge(sem_add, h + 1)
                    settle(dve, "sp")
                    for b in range(2):
                        v.bn_stats(stats[:, ds(h * 2 + b, 1), :].rearrange("p a b -> p (a b)"), X[:, ds(h * 2 + b, 1), 0:F].rearrange("p a b -> p (a b)")).then_inc(sem_bn, 1)
                return f

            def moments(sem_bn, ready):
                dve.wait_ge(sem_bn, BLOCKS)
                me, ve, mo, vo = (stats[:, :, k] for k in (1, 2, 4, 5))
                chain(v.tensor_tensor(tmp[:, :], me, mo, ALU.subtract))
                chain(v.tensor_tensor(mean[:, :], me, mo, ALU.add))
                chain(v.tensor_tensor(var[:, :], ve, vo, ALU.add))
                chain(v.tensor_tensor(tmp[:, :], tmp[:, :], tmp[:, :], ALU.mult))
                chain(v.tensor_scalar(mean[:, :], mean[:, :], 0.5, None, ALU.mult))
                chain(v.tensor_scalar(tmp[:, :], tmp[:, :], 0.25, None, ALU.mult))
                v.scalar_tensor_tensor(out=var[:, :], in0=var[:, :], scalar=1.0 / F, in1=tmp[:, :], op0=ALU.mult, op1=ALU.add).then_inc(ready, 1)

            def scales(sq):
                dve.wait_ge(sq, 1)
                chain(v.reciprocal(rstd[:, :], tmp[:, :]))
                chain(v.scalar_tensor_tensor(out=nmr[:, :], in0=mean[:, :], scalar=-1.0, in1=rstd[:, :], op0=ALU.mult, op1=ALU.mult))

            dve.wait_ge(x_in, 32)
            over(dve, HALVES - 1, [(0, add_to_x(n1_tr, n1_add)), (1, row_stats(n1_add, n1_bn))])
            moments(n1_bn, stat_ok)
            scales(sq_ok)

            def normalise(h, p, w):
                after(dve, cp_ok, h - 1)
                after(dve, n1_t2, h - 1)
                after(dve, ls_ok, 2 * h - 2)
                for b in range(2):
                    v.tensor_scalar(stg[p][:, b * 128:(b + 1) * 128], X[:, ds(h * 2 + b, 1), 0:F].rearrange("p a b -> p (a b)"),
                                    rstd[:, ds(h * 2 + b, 1)], nmr[:, ds(h * 2 + b, 1)], ALU.mult, ALU.add).then_inc(nm_ok, 1)

            def src_logit(h, p, w):
                dve.wait_ge(nm_ok, 2 * h + 2)
                after(dve, ls_ok, 2 * h - 2)
                for b in range(2):
                    v.scalar_tensor_tensor(out=junk[:, 2 * p + b, :], in0=stg[p][:, b * 128:(b + 1) * 128], scalar=1.0, in1=wsrc_row[:, :],
                                           op0=ALU.mult, op1=ALU.mult,
                                           accum_out=X[:, ds(h * 2 + b, 1), F:F + 1].rearrange("p a b -> p (a b)")).then_inc(ls_ok, 1)

            over(dve, HALVES - 1, [(0, normalise), (1, src_logit)])

            def dst_logit(q, s, j):
                t = q * SC + j
                a = dve.value_load(base[0:1, ds(t, 1)], min_val=0, max_val=NP - 128)
                after(dve, ld_ok, t - 3)
                v.scalar_tensor_tensor(out=junk[:, (s * SC + j) % 4, :], in0=iota_n[:, :], scalar=relT[:, ds(t, 1)], in1=ldbc[:, ds(a, 128)],
                                       op0=ALU.is_equal, op1=ALU.mult, accum_out=ldE[:, s, j:j + 1]).then_inc(ld_ok, 1)

            def softmax(i, s):
                q = i * 2 + s
                dve.wait_ge(rows_landed[s], (i + 1) * (16 * SC))
                dve.wait_ge(ld_ok, (q + 1) * SC)
                after(dve, lg_tr, q)
                v.tensor_tensor(zE[:, :], G[:, s * SC:(s + 1) * SC, F], ldE[:, s, :], ALU.add).then_inc(lg_ok, 1)
                dve.wait_ge(lg_ok, 2 * q + 1)
                v.scalar_tensor_tensor(out=lgE[:, :], in0=zE[:, :], scalar=SLOPE, in1=zE[:, :], op0=ALU.mult, op1=ALU.max).then_inc(lg_ok, 1)
                dve.wait_ge(lg_tr, q + 1)
                dve.wait_ge(meta_in[s], i * 16 + 16)
                after(dve, last_tr, q)
                logits = bank[4][0:SC, 0:T]
                starts, finishes, others = (mt[0:SC, s, k, :] for k in range(3))
                v.tensor_tensor_scan(out=fw[0:SC, :], data0=starts, data1=logits, initial=NEG, op0=ALU.add, op1=ALU.max).then_inc(sc_ok, 1)
                v.tensor_tensor_scan(out=bk[0:SC, ::-1], data0=finishes[:, ::-1], data1=logits[:, ::-1], initial=NEG, op0=ALU.add, op1=ALU.max).then_inc(sc_ok, 1)
                after(dve, run_tr, q - 1)
                v.tensor_copy(run[0:1, s, 0:1], run[0:1, 1 - s, SC:SC + 1]).then_inc(run_ok, 1)
                dve.wait_ge(sc_ok, 3 * q + 2)
                v.tensor_tensor(mM[0:SC, :], fw[0:SC, :], bk[0:SC, :], ALU.max).then_inc(sc_ok, 1)
                dve.wait_ge(last_tr, q + 1)
                dve.wait_ge(run_ok, 2 * q + 1)
                v.tensor_tensor_scan(out=run[0:1, s, 1:SC + 1], data0=cont[:, ds(q * SC, SC)], data1=bank[5][0:1, 0:SC],
                                     initial=run[0:1, s, 0:1], op0=ALU.add, op1=ALU.max).then_inc(run_ok, 1)
                dve.wait_ge(run_tr, q + 1)
                v.tensor_tensor(carry[0:SC, :], bank[6][0:SC, 0:1], starts[:, 0:1], ALU.add).then_inc(cr, 1)
                dve.wait_ge(cr, 3 * q + 1)
                dve.wait_ge(sc_ok, 3 * q + 3)
                v.scalar_tensor_tensor(out=mM[0:SC, :], in0=others, scalar=carry[0:SC, :], in1=mM[0:SC, :], op0=ALU.add, op1=ALU.max).then_inc(cr, 1)
                dve.wait_ge(cr, 3 * q + 2)
                after(dve, exp_ok, q)
                v.tensor_tensor(dif[0:SC, T:T + 1], carry[0:SC, :], mM[0:SC, 0:1], ALU.subtract).then_inc(cr, 1)
                dve.wait_ge(cr, 3 * q + 3)
                v.tensor_tensor(dif[0:SC, 0:T], logits, mM[0:SC, :], ALU.subtract).then_inc(dif_ok, 1)

            def weigh(q, s, j):
                t = q * SC + j
                if j == 0:
                    dve.wait_ge(ev_ok, q + 1)
                after(dve, t_mm, t - 3)
                v.tensor_scalar(A[:, (s * SC + j) % 4, :], iota_n[:, :], relT[:, ds(t, 1)], evr[:, s, 0, j:j + 1],
                                ALU.is_equal, ALU.mult).then_inc(a_ok, 1)

            def sum_up(q, s, j):
                t = q * SC + j
                a = dve.value_load(base[0:1, ds(t, 1)], min_val=0, max_val=NP - 128)
                win = cacc[:, :, ds(a, 128)]
                dve.wait_ge(t_mm, t + 1)
                after(dve, sum_ok, t)
                v.scalar_tensor_tensor(out=win, in0=win, scalar=evr[:, s, 1, j:j + 1],
                                       in1=bank[(s * SC + j) % 4][:, 0:256].rearrange("p (a n) -> p a n", a=2),
                                       op0=ALU.mult, op1=ALU.add).then_inc(sum_ok, 1)

            def second(i, last=False):
                for s in range(2):
                    q = i * 2 + s
                    softmax(i, s)
                    for j in range(SC + 2):
                        if j < SC:
                            weigh(q, s, j)
                            if not (last and s == 1):
                                dst_logit(q + 1, 1 - s, j)
                        if j >= 2:
                            sum_up(q, s, j - 2)

            dve.wait_ge(ldb_ok, HALVES)
            dve.wait_ge(ls_ok, BLOCKS)
            dve.wait_ge(cleared, 2)
            for j in range(SC):
                dst_logit(0, 0, j)
            second(0)
            with dve.Fori(1, PASSES - 1) as i:
                second(i)
            second(PASSES - 1, last=True)

            def ratio(c, p, w):
                settle(dve, "sp")
                v.reciprocal(rec[p][:, 0:w], cacc[:, 1, ds(c * CH, w)]).then_inc(y_ok, 1)
                dve.wait_ge(y_ok, 2 * c + 1)
                after(dve, c_mm, c - 1)
                v.tensor_tensor(Y[p][:, 0:w], cacc[:, 0, ds(c * CH, w)], rec[p][:, 0:w], ALU.mult).then_inc(y_ok, 1)

            def signs(c, p, w):
                dve.wait_ge(c_mm, c + 1)
                after(dve, ctx_ok, c - 1)
                v.tensor_scalar(mx[p][:, 0:w], bank[p][:, 0:w], BP, 0.0, ALU.add, ALU.max)
                v.tensor_scalar(mn[p][:, 0:w], bank[p][:, 0:w], BP, 0.0, ALU.add, ALU.min).then_inc(mm_ok, 1)

            def elu(c, p, w):
                dve.wait_ge(ex_ok, c + 1)
                dve.wait_ge(mm_ok, c + 1)
                after(dve, h1_mm, c - 1)
                v.scalar_tensor_tensor(out=ctxb[p][:, 0:w], in0=ex[p][:, 0:w], scalar=-1.0, in1=mx[p][:, 0:w], op0=ALU.add, op1=ALU.add).then_inc(ctx_ok, 1)

            def col_stats(c, p, w):
                dve.wait_ge(h2_ok, c + 1)
                settle(dve, "sp")
                v.bn_stats(bnst[:, ds(c, 1), :].rearrange("p a b -> p (a b)"), H[:, ds(c * CH, w)]).then_inc(bn_ok, 1)

            dve.wait_ge(sum_ok, TILES)
            over(dve, CHUNKS, [(0, ratio), (0, signs), (1, elu), (3, col_stats)], width=CH, tail=N - CHUNKS * CH)
            dve.wait_ge(bn_ok, CHUNKS + 1)
            v.bn_aggr(bnmv[:, :], bnst[:, :, :].rearrange("p a b -> p (a b)")).then_inc(aff_ok, 2)
            dve.wait_ge(aff_ok, 3)
            v.reciprocal(scl[:, :], scl[:, :]).then_inc(aff_ok, 1)
            dve.wait_ge(aff_ok, 4)
            v.tensor_tensor(scl[:, :], scl[:, :], GAM, ALU.mult).then_inc(aff_ok, 1)
            dve.wait_ge(aff_ok, 5)
            v.scalar_tensor_tensor(out=shf[:, :], in0=bnmv[:, 0:1], scalar=-1.0, in1=scl[:, :], op0=ALU.mult, op1=ALU.mult).then_inc(aff_ok, 1)
            dve.wait_ge(aff_ok, 6)
            v.tensor_tensor(shf[:, :], shf[:, :], BET, ALU.add).then_inc(aff_ok, 1)

            over(dve, HALVES - 1, [(0, add_to_x(n2_tr, n2_add)), (1, row_stats(n2_add, n2_bn))])
            moments(n2_bn, stat2_ok)
            scales(sq2_ok)

            def finish(h, p, w):
                after(dve, out_done[p], (h - p) * 8)
                for b in range(2):
                    v.tensor_scalar(outs[p][:, b, :], X[:, ds(h * 2 + b, 1), 0:F].rearrange("p a b -> p (a b)"),
                                    rstd[:, ds(h * 2 + b, 1)], nmr[:, ds(h * 2 + b, 1)], ALU.mult, ALU.add).then_inc(nm2_ok, 1)

            over(dve, HALVES - 1, [(0, finish)])


_INS = ['x', 'src', 'dst', 'L0_gnn_W1', 'L0_gnn_b1', 'L0_gnn_W2', 'L0_gnn_b2', 'L0_gnn_W3', 'L0_gnn_b3',
        'L1_gnn_we_dst', 'L1_gnn_we_src', 'L1_gnn_be', 'L1_gnn_w_proj', 'L1_gnn_b_proj', 'L1_gnn_w1', 'L1_gnn_b1',
        'L1_gnn_w2', 'L1_gnn_b2', 'L1_gnn_gamma', 'L1_gnn_beta']


def kernel(**inputs):
    import numpy as _np
    import concourse.bacc as _bacc
    from concourse import mybir as _mybir
    from concourse.bass_utils import run_bass_kernel_spmd as _run

    nc = _bacc.Bacc("TRN2", target_bir_lowering=False, num_devices=1)
    arrays, args = {}, []
    for name in _INS:
        a = _np.ascontiguousarray(inputs[name])
        arrays[f"in_{name}"] = a
        args.append(nc.dram_tensor(f"in_{name}", a.shape, _mybir.dt.from_np(a.dtype), kind="ExternalInput").ap())
    args.append(nc.dram_tensor("out_0", (N, F), _mybir.dt.float32, kind="ExternalOutput").ap())
    build(nc, *args)
    r = _run(nc, [arrays], core_ids=[0])
    return r.results[0]["out_0"]
```

```python
import concourse.bass as bass
from concourse import mybir
from contextlib import ExitStack

N = 6250
E = 206250
F = 128
T = 128
TILES = -(-E // T)
PASS = 52
PASSES = TILES // PASS
GT = 4
GROUPS = PASS // GT
SC = PASS // 2
HC = SC // 2
LD = HC
ROWS = 124
COLS = TILES // ROWS
HALVES = 25
BLOCKS = 2 * HALVES
NP = BLOCKS * 128
LAST = N - (BLOCKS - 2) * 128
TAB = 132
CH = 512
CHUNKS = N // CH
EPS = 1e-5
SLOPE = 0.01
NEG = -1.0e38
assert TILES == PASS * PASSES == ROWS * COLS and PASS == GT * GROUPS


def build(nc, x, src, dst, W1, b1, W2, b2, W3, b3, we_dst, we_src, be, w_proj, b_proj,
          w1, bb1, w2, bb2, gamma, beta, out):
    fp32, bf16, i32 = mybir.dt.float32, mybir.dt.bfloat16, mybir.dt.int32
    ALU, ACT = mybir.AluOpType, mybir.ActivationFunctionType
    ds = bass.ds
    nc.disable_value_cache = True

    p_tab = nc.dram_tensor("p_tab", (NP, F), fp32, kind="Internal").ap()
    q_tab = nc.dram_tensor("q_tab", (NP, F), fp32, kind="Internal").ap()
    x1_tab = nc.dram_tensor("x1_tab", (NP, TAB), fp32, kind="Internal").ap()
    meta = nc.dram_tensor("meta", (4, TILES * T), bf16, kind="Internal").ap()
    ld_d = nc.dram_tensor("ld_d", (1, NP), fp32, kind="Internal").ap()
    cont_d = nc.dram_tensor("cont_d", (1, TILES), fp32, kind="Internal").ap()

    ctx = ExitStack()
    with ctx:
        def sb(name, shape, dt=fp32):
            return ctx.enter_context(nc.sbuf_tensor(name, shape, dt))

        def sem(name):
            return ctx.enter_context(nc.semaphore(name))

        ident, iota_n, ones = sb("ident", [128, 128]), sb("iota_n", [128, 128]), sb("ones", [128, 128])
        den_row = sb("den_row", [128, 128])
        W1s, W2s, Wpq, W3s = sb("W1s", [128, 128]), sb("W2s", [128, 2, 128]), sb("Wpq", [128, 2, 128]), sb("W3s", [128, 128])
        wprojs, w1s, w2s = sb("wprojs", [128, 128]), sb("w1s", [128, 2, 128]), sb("w2s", [128, 128])
        brow = sb("brow", [128, 2, 128])
        wsrc_row = sb("wsrc_row", [128, 128])
        wproj0 = sb("wproj0", [128, 128])
        cols = sb("cols", [128, 9])
        B1, B3, BB1, BB2, GAM, BET, WDST, BE, neg_p = (cols[:, i:i + 1] for i in range(9))
        srcT, relT, endT = sb("srcT", [128, TILES], i32), sb("relT", [128, TILES]), sb("endT", [128, TILES])
        rows = sb("rows", [128, TILES])
        cont = rows[0:1, :]
        base = rows[64:65, :].bitcast(i32)
        idx = sb("idx", [128, PASS], i32)
        X = sb("X", [128, BLOCKS, TAB])
        accT = sb("accT", [128, NP])
        G = sb("G", [128, PASS, TAB])
        ZW = 21760
        Z = sb("Z", [128, ZW])
        stats = sb("stats", [128, BLOCKS, 6])
        mean, var, rstd, nmr, tmp = (sb(n, [128, BLOCKS]) for n in ("mean", "var", "rstd", "nmr", "tmp"))
        bnst, bnmv = sb("bnst", [128, CHUNKS + 1, 6]), sb("bnmv", [128, 2])
        scl, shf, eps = sb("scl", [128, 1]), sb("shf", [128, 1]), sb("eps", [128, 1])

        top = [0]

        def z(shape, dt=fp32):
            n = 1
            for s in shape:
                n *= s
            words = n if dt != bf16 else n // 2
            assert top[0] + words <= ZW
            part = Z[:, top[0]:top[0] + words]
            top[0] += words
            assert top[0] <= ZW, top[0]
            if dt != fp32:
                part = part.bitcast(dt)
            if len(shape) == 2:
                part = part.rearrange("p (a b) -> p a b", a=shape[0])
            if len(shape) == 3:
                part = part.rearrange("p (a b c) -> p a b c", a=shape[0], b=shape[1])
            return part

        D = z([COLS, T + 2], i32)
        S0 = z([COLS, T], i32)
        srcF, rel, relend, flag = z([COLS, T]), z([COLS, T]), z([COLS, T]), z([COLS, T])
        metaS = z([4, COLS, T], bf16)
        contS = z([COLS])
        xin = [z([2, 128]) for _ in range(2)]
        xTs = [z([256]) for _ in range(2)]
        hTs = [z([256]) for _ in range(2)]
        pqs = [z([2, 256]) for _ in range(2)]
        top[0] = 0
        Pwin = z([PASS, 128])
        bc = z([2, PASS * T], bf16)
        SQ = [z([CH], bf16) for _ in range(3)]
        OH = [z([CH]) for _ in range(3)]
        M1 = [z([CH]) for _ in range(3)]
        S = [z([CH]) for _ in range(3)]
        STs = [z([CH]) for _ in range(3)]
        EOH = [z([GT, 128]) for _ in range(3)]
        top[0] = 0
        cacc = z([NP])
        H = cacc
        z2 = top[0]
        near = z([2, SC * T], bf16)
        SQ2 = z([HC * T], bf16)
        OH2 = [z([HC * T]) for _ in range(2)]
        EQ = [z([HC, 128]) for _ in range(2)]
        LWd = z([2, SC * SC])
        Gs = [z([128]) for _ in range(4)]
        LW = z([2, 128])
        mts = [z([3, T], bf16) for _ in range(2)]
        fw, bk, mM, low, lg = (z([T]) for _ in range(5))
        dif, exd = z([T + 1]), z([T + 1])
        top[0] = z2
        rec, Y, mn, mx, ex, ctxb, h1 = ([z([CH]) for _ in range(2)] for _ in range(7))
        outs = [z([2, 128]) for _ in range(2)]
        stg = [sb(f"stg{i}", [128, 256]) for i in range(2)]
        lrow = sb("lrow", [128, 2, 256])
        run = sb("run", [128, 2, SC + 1])
        carry = sb("carry", [128, 1])
        evr = sb("evr", [128, 2, 2, SC])
        junk = sb("junk", [128, 4, 128], bf16)

        bank = [ctx.enter_context(nc.psum_tensor(f"bank{i}", [128, 512], fp32)) for i in range(8)]

        weights_in, x_in, lists_in, base_in, rows_in = (sem(n) for n in ("weights_in", "x_in", "lists_in", "base_in", "rows_in"))
        consts, pads, prep = sem("consts"), sem("pads"), sem("prep")
        xin_in = [sem(f"xin_in{i}") for i in range(2)]
        xt_tr, xt_cp, h_mm, h_ev, pq_mm, pq_ev = (sem(n) for n in ("xt_tr", "xt_cp", "h_mm", "h_ev", "pq_mm", "pq_ev"))
        pq_out = [sem(f"pq_out{i}") for i in range(2)]
        meta_out, cont_out, list_tr, list_ev = sem("meta_out"), sem("cont_out"), sem("list_tr"), sem("list_ev")
        idx_ok = sem("idx_ok")
        landed = [sem(f"landed{g}") for g in range(GROUPS)]
        win_in = [sem(f"win_in{g}") for g in range(GROUPS)]
        bc_in = [sem(f"bc_in{i}") for i in range(2)]
        dist_ok, oh_ok, x_mm, relu_ok, v_mm, scan_ok, s_tr, st_ok, eoh_ok, o_mm, acc_ok = (sem(n) for n in (
            "dist_ok", "oh_ok", "x_mm", "relu_ok", "v_mm", "scan_ok", "s_tr", "st_ok", "eoh_ok", "o_mm", "acc_ok"))
        n1_st, n1_tr, n1_add, n1_bn, stat_ok, sq_ok = (sem(n) for n in ("n1_st", "n1_tr", "n1_add", "n1_bn", "stat_ok", "sq_ok"))
        nm_ok, ls_ok, cp_ok, n1_t2, x1t_ok, ld_mm, ldb_ok, tab_out = (sem(n) for n in (
            "nm_ok", "ls_ok", "cp_ok", "n1_t2", "x1t_ok", "ld_mm", "ldb_ok", "tab_out"))
        cleared = sem("cleared")
        meta_in = [sem(f"meta_in{i}") for i in range(2)]
        rows_landed = [sem(f"rows_landed{i}") for i in range(2)]
        ld_put, lw_tr, lw_ok, near_in, lw_in = [sem(f"ld_put{i}") for i in range(2)], sem("lw_tr"), sem("lw_ok"), [sem(f"near_in{i}") for i in range(2)], [sem(f"lw_in{i}") for i in range(2)]
        sq2_a, oh2_ok, z_ld, z_mm, low_ok, lg_ok, sc_ok, last_tr, run_ok, run_tr, cr, dif_ok, exp_ok, ev_tr, ev_ok = (sem(n) for n in (
            "sq2_a", "oh2_ok", "z_ld", "z_mm", "low_ok", "lg_ok", "sc_ok", "last_tr", "run_ok", "run_tr", "cr", "dif_ok", "exp_ok", "ev_tr", "ev_ok"))
        eq_ok, gs_ok, t_mm, sum_ok = sem("eq_ok"), sem("gs_ok"), sem("t_mm"), sem("sum_ok")
        y_ok, c_mm, mm_ok, ex_ok, ctx_ok, h1_mm, h1_ok, h2_mm, h2_ok, bn_ok = (sem(n) for n in (
            "y_ok", "c_mm", "mm_ok", "ex_ok", "ctx_ok", "h1_mm", "h1_ok", "h2_mm", "h2_ok", "bn_ok"))
        aff_ok, n2_st, n2_tr, n2_add, n2_bn, stat2_ok, sq2_ok, nm2_ok = (sem(n) for n in (
            "aff_ok", "n2_st", "n2_tr", "n2_add", "n2_bn", "stat2_ok", "sq2_ok", "nm2_ok"))
        out_done = [sem(f"out_done{i}") for i in range(2)]
        turns = {e: sem(f"turns_{e}") for e in ("pool", "act", "dve", "pe", "sp")}

        def after(eng, s, n):
            if not isinstance(n, int) or n > 0:
                eng.wait_ge(s, n)

        def settle(eng, name):
            eng.sem_inc(turns[name], 1)

        def over(eng, full, stages, width=None, tail=None):
            lag = max(k for k, _ in stages)
            first = 4

            def step(h, p, static):
                for k, f in stages:
                    if static and not 0 <= h - k <= full:
                        continue
                    f(h - k, (p - k) % 2, tail if static and h - k == full else width)

            for h in range(first):
                step(h, h % 2, True)
            assert lag <= first and full % 2 == 0
            with eng.Fori(first // 2, full // 2) as i:
                step(i * 2, 0, False)
                step(i * 2 + 1, 1, False)
            for h in range(full, full + 1 + lag):
                step(h, h % 2, True)

        def groups(eng, stages):
            def a_pass(i, upto=GROUPS):
                for g in range(upto):
                    for k, f in stages:
                        gg, ii = (g - k, i) if g >= k else (g - k + GROUPS, i - 1)
                        if isinstance(i, int) and (ii < 0 or ii >= PASSES):
                            continue
                        f(ii * GROUPS + gg, gg, ii)

            a_pass(0)
            with eng.Fori(1, PASSES) as i:
                a_pass(i)
            a_pass(PASSES, max(k for k, _ in stages))

        def bases(engine, t, n):
            _, got = nc.values_load_multi_w_load_instructions(base[0:1, ds(t, n)], engines=(engine,), min_val=0, max_val=NP - 128,
                                                             skip_runtime_bounds_check_because="a destination is a node, so below N")
            return got

        def used2(k, g):
            return k if g == 0 else k - 1

        def ring(g):
            return 2 if g == GROUPS - 1 else g % 2

        block = ctx.enter_context(nc.Block())

        @block.sync
        def _(sp):
            for to, of in ((W1s[:, :], W1[:, :]), (W2s[:, :, :], W2.rearrange("(a k) n -> k a n", a=2)),
                           (W3s[:, :], W3[:, :]), (wprojs[0:127, :], w_proj[1:128, :]),
                           (wprojs[127:128, :], b_proj.rearrange("(a n) -> a n", a=1)), (wproj0[:, :], w_proj[0:1, :].broadcast_to([128, 128])),
                           (w1s[:, :, :], w1.rearrange("(a k) n -> k a n", a=2)), (w2s[:, :], w2[:, :]),
                           (brow[:, 0, :], b2.rearrange("(a n) -> a n", a=1).broadcast_to([128, 128])),
                           (wsrc_row[:, :], we_src.rearrange("(a n) -> a n", a=1).broadcast_to([128, 128]))):
                sp.dma_start(to, of).then_inc(weights_in, 16)
            with nc.allow_non_contiguous_dma(reason="a few vectors"):
                for to, of in ((B1, b1), (B3, b3), (BB1, bb1), (BB2, bb2), (GAM, gamma),
                               (BET, beta), (WDST, we_dst)):
                    sp.dma_start(to, of.rearrange("(n a) -> n a", a=1)).then_inc(weights_in, 16)
                sp.dma_start(BE, be.rearrange("(n a) -> n a", a=1).broadcast_to([128, 1])).then_inc(weights_in, 16)
                sp.dma_start(base[:, 0:TILES - 1], dst[0:(TILES - 1) * T].rearrange("(t e) -> e t", e=T)[0:1, :]).then_inc(base_in, 16)
                sp.dma_start(base[:, TILES - 1:TILES], dst[(TILES - 1) * T:(TILES - 1) * T + 1].rearrange("(a n) -> a n", a=1)).then_inc(base_in, 16)
            sp.wait_ge(pads, 5)
            sp.dma_start(X[:, 0:BLOCKS - 2, 0:F], x[0:(BLOCKS - 2) * 128, :].rearrange("(b p) f -> p b f", p=128)).then_inc(x_in, 16)
            sp.dma_start(X[0:LAST, BLOCKS - 2, 0:F], x[(BLOCKS - 2) * 128:N, :]).then_inc(x_in, 16)

            def load_x(h, p, w):
                after(sp, xt_tr, h - 1)
                settle(sp, "sp")
                if w:
                    sp.dma_start(xin[p][0:LAST, 0, :], x[(BLOCKS - 2) * 128:N, :]).then_inc(xin_in[p], 16)
                else:
                    sp.dma_start(xin[p], x[ds(h * 256, 256), :].rearrange("(b p) f -> p b f", p=128)).then_inc(xin_in[p], 16)

            def store_pq(h, p, w):
                sp.wait_ge(pq_ev, h + 1)
                settle(sp, "sp")
                for tab, o in ((p_tab, 0), (q_tab, 128)):
                    sp.dma_start(tab[ds(h * 256, 256), :].rearrange("(b p) f -> p b f", p=128),
                                 pqs[p][:, :, o:o + 128]).then_inc(pq_out[p], 16)

            over(sp, HALVES - 1, [(0, load_x), (3, store_pq)], tail=1)

            sp.wait_ge(prep, 7)
            for k in range(4):
                sp.dma_start(meta[k, :].rearrange("(c p e) -> p c e", p=ROWS, e=T), metaS[0:ROWS, k]).then_inc(meta_out, 16)
            with nc.allow_non_contiguous_dma(reason="one number for each tile"):
                sp.dma_start(cont_d[0, :].rearrange("(c p) -> p c", p=ROWS), contS[0:ROWS, :]).then_inc(cont_out, 16)
            sp.wait_ge(cont_out, 16)
            sp.dma_start(cont, cont_d[:, :]).then_inc(rows_in, 16)
            sp.wait_ge(meta_out, 64)
            sp.wait_ge(base_in, 32)
            sp.wait_ge(pq_out[0], 32 * 13)
            sp.wait_ge(pq_out[1], 32 * 12)
            sp.wait_ge(cont_out, 16)
            sp.wait_ge(list_tr, 3 * COLS)

            def windows(i, g):
                at = bases(mybir.EngineType.SP, i * PASS + g * GT, GT)
                after(sp, x_mm, (i - 1) * GROUPS + g + 1)
                settle(sp, "sp")
                for j in range(GT):
                    sp.dma_start(Pwin[:, g * GT + j, :], p_tab[ds(at[j], 128), :]).then_inc(win_in[g], 16)

            def spread(i, half):
                a, b = ((0, 7), (7, GROUPS))[half]
                after(sp, scan_ok, (i - 1) * GROUPS + b)
                after(sp, dist_ok, (i - 1) * GROUPS + b)
                settle(sp, "sp")
                for k in range(2):
                    sp.dma_start(bc[:, k, a * CH:b * CH],
                                 meta[k:k + 1, ds(i * (PASS * T) + a * CH, (b - a) * CH)].broadcast_to([128, (b - a) * CH])).then_inc(bc_in[half], 16)

            def first_layer(i):
                spread(i, 0)
                for g in range(7):
                    windows(i, g)
                spread(i, 1)
                for g in range(7, GROUPS):
                    windows(i, g)

            first_layer(0)
            with sp.Fori(1, PASSES) as i:
                first_layer(i)

            def store_tab(h, p, w):
                sp.wait_ge(cp_ok, h + 1)
                sp.wait_ge(ls_ok, 2 * h + 2)
                settle(sp, "sp")
                sp.dma_start(x1_tab[ds(h * 256, 256), :].rearrange("(b p) f -> p b f", p=128), X[:, ds(h * 2, 2), :]).then_inc(tab_out, 16)

            def store_ld(h, p, w):
                sp.wait_ge(ldb_ok, h + 1)
                settle(sp, "sp")
                sp.dma_start(ld_d[:, ds(h * 256, 256)], lrow[0:1, p, :]).then_inc(ld_put[p], 16)

            over(sp, HALVES - 1, [(0, store_tab), (1, store_ld)])

            sp.wait_ge(ld_put[0], 16 * 13)
            sp.wait_ge(ld_put[1], 16 * 12)

            def load_group(i, s):
                q = i * 2 + s
                after(sp, dif_ok, q - 1)
                settle(sp, "sp")
                after(sp, sq2_a, 2 * (q - 1))
                settle(sp, "sp")
                after(sp, lw_tr, q - 1)
                settle(sp, "sp")
                sp.dma_start(mts[s][0:SC], meta[1:4, ds(q * (SC * T), SC * T)].rearrange("k (t e) -> t k e", e=T)).then_inc(meta_in[s], 16)
                sp.dma_start(near[:, s, :], meta[0:1, ds(q * (SC * T), SC * T)].broadcast_to([128, SC * T])).then_inc(near_in[s], 16)
                for c in range(2):
                    at = bases(mybir.EngineType.SP, q * SC + c * HC, HC)
                    for j in range(HC):
                        sp.dma_start(LW[c * HC + j:c * HC + j + 1, s, :], ld_d[0:1, ds(at[j], 128)]).then_inc(lw_in[s], 16)

            for s in range(2):
                load_group(0, s)
            with sp.Fori(1, PASSES) as i:
                for s in range(2):
                    load_group(i, s)

            def store_out(h, p, w):
                sp.wait_ge(nm2_ok, 2 * h + 2)
                settle(sp, "sp")
                if w:
                    sp.dma_start(out[(BLOCKS - 2) * 128:N, :], outs[p][0:LAST, 0, :]).then_inc(out_done[p], 16)
                else:
                    sp.dma_start(out[ds(h * 256, 256), :].rearrange("(b p) f -> p b f", p=128), outs[p]).then_inc(out_done[p], 16)

            over(sp, HALVES - 1, [(0, store_out)], tail=1)
            sp.wait_ge(out_done[0], 16 * 13)
            sp.wait_ge(out_done[1], 16 * 12)

        @block.gpsimd
        def _(pool):
            nc.gpsimd.memset(ident[:, :], 0.0).then_inc(turns["pool"], 1)
            nc.gpsimd.memset(D[:, :, :], -1).then_inc(pads, 1)
            nc.gpsimd.memset(S0[:, :, :], 0).then_inc(pads, 1)
            nc.gpsimd.memset(X[:, BLOCKS - 2:BLOCKS, 0:F], 0.0).then_inc(pads, 1)
            nc.gpsimd.memset(X[:, :, F + 1:TAB], 0.0).then_inc(pads, 1)
            nc.gpsimd.memset(X[:, :, F:F + 1], 1.0).then_inc(pads, 1)
            nc.gpsimd.iota(iota_n[:, :], pattern=[[1, 128]], base=0, channel_multiplier=0, allow_small_or_imprecise_dtypes=True).then_inc(consts, 1)
            nc.gpsimd.iota(neg_p, pattern=[[0, 1]], base=0, channel_multiplier=-1, allow_small_or_imprecise_dtypes=True).then_inc(consts, 1)
            nc.gpsimd.memset(ones[:, :], 1.0).then_inc(consts, 1)
            nc.gpsimd.memset(eps[:, :], EPS).then_inc(consts, 1)
            nc.gpsimd.memset(run[:, :, :], NEG).then_inc(consts, 1)
            nc.gpsimd.memset(brow[:, 1, :], 0.0).then_inc(consts, 1)
            pool.wait_ge(turns["pool"], 1)
            nc.gpsimd.affine_select(out=ident[:, :], in_=ident[:, :], compare_op=ALU.not_equal, fill=1.0, base=0,
                                    pattern=[[-1, 128]], channel_multiplier=1).then_inc(consts, 1)
            pool.wait_ge(pads, 2)
            whole = ROWS * T
            end = (COLS - 1) * whole
            pool.dma_start(D[0:1, 0, 1:T + 2], dst[0:T + 1].rearrange("(a n) -> a n", a=1)).then_inc(lists_in, 16)
            pool.dma_start(D[1:ROWS, 0, 0:T + 2], bass.AP(dst.tensor, T - 1, [[T, ROWS - 1], [1, T + 2]])).then_inc(lists_in, 16)
            pool.dma_start(D[0:ROWS, 1:COLS - 1, 0:T + 2], bass.AP(dst.tensor, whole - 1, [[T, ROWS], [whole, COLS - 2], [1, T + 2]])).then_inc(lists_in, 16)
            pool.dma_start(D[0:ROWS - 1, COLS - 1, 0:T + 2], bass.AP(dst.tensor, end - 1, [[T, ROWS - 1], [1, T + 2]])).then_inc(lists_in, 16)
            pool.dma_start(D[ROWS - 1:ROWS, COLS - 1, 0:E - (TILES - 1) * T + 1], dst[(TILES - 1) * T - 1:E].rearrange("(a n) -> a n", a=1)).then_inc(lists_in, 16)
            pool.dma_start(S0[0:ROWS, 0:COLS - 1, :], src[0:end].rearrange("(c p e) -> p c e", p=ROWS, e=T)).then_inc(lists_in, 16)
            pool.dma_start(S0[0:ROWS - 1, COLS - 1, :], src[end:(TILES - 1) * T].rearrange("(p e) -> p e", e=T)).then_inc(lists_in, 16)
            pool.dma_start(S0[ROWS - 1:ROWS, COLS - 1, 0:E - (TILES - 1) * T], src[(TILES - 1) * T:E].rearrange("(a n) -> a n", a=1)).then_inc(lists_in, 16)
            nc.gpsimd.memset(accT[:, :], 0.0).then_inc(cleared, 1)

            half = PASS // 2

            def indices(i, s, free):
                for f, n in free:
                    after(pool, f, n)
                settle(pool, "pool")
                nc.gpsimd.tensor_copy(idx[:, s * half:(s + 1) * half], srcT[:, ds(i * PASS + s * half, half)]).then_inc(idx_ok, 1)

            pool.wait_ge(list_ev, 12)
            pool.wait_ge(pq_out[0], 32 * 13)
            pool.wait_ge(pq_out[1], 32 * 12)

            def gather_q(i):
                indices(i, 0, [(landed[g], i * 64) for g in range(7)])
                pool.wait_ge(idx_ok, i * 2 + 1)
                for g in range(GROUPS):
                    if g == 6:
                        indices(i, 1, [(landed[u], i * 64) for u in range(7, GROUPS)] + [(landed[6], i * 64)])
                        pool.wait_ge(idx_ok, i * 2 + 2)
                    after(pool, x_mm, (i - 1) * GROUPS + g + 1)
                    settle(pool, "pool")
                    for j in range(g * GT, g * GT + GT):
                        pool.indirect_dma_start(G[:, j, 0:F], None, q_tab[:, :],
                                                bass.IndirectOffsetOnAxis(ap=idx[:, j:j + 1], axis=0)).then_inc(landed[g], 16)

            gather_q(0)
            with pool.Fori(1, PASSES) as i:
                gather_q(i)

            pool.wait_ge(acc_ok, TILES)
            nc.gpsimd.memset(cacc, 0.0).then_inc(cleared, 1)
            nc.gpsimd.memset(LWd, 0.0).then_inc(cleared, 1)
            for g in range(GROUPS):
                pool.wait_ge(landed[g], 64 * PASSES)
            pool.wait_ge(tab_out, 16 * HALVES)

            def gather_x1(i):
                for s in range(2):
                    indices(i, s, [(rows_landed[s], i * (16 * SC))])
                    pool.wait_ge(idx_ok, (i + PASSES) * 2 + s + 1)
                    for j in range(SC):
                        if j % HC == 0:
                            after(pool, gs_ok, (i - 1) * PASS + s * SC + j + HC)
                            after(pool, z_mm, i * 2 + s - 1)
                            settle(pool, "pool")
                        u = s * SC + j
                        pool.indirect_dma_start(G[:, u, :], None, x1_tab[:, :],
                                                bass.IndirectOffsetOnAxis(ap=idx[:, u:u + 1], axis=0)).then_inc(rows_landed[s], 16)

            gather_x1(0)
            with pool.Fori(1, PASSES) as i:
                gather_x1(i)

        @block.scalar
        def _(act):
            act.wait_ge(weights_in, 16 * 18)
            act.wait_ge(consts, 7)

            def h_evac(h, p, w):
                act.wait_ge(h_mm, h + 1)
                after(act, pq_mm, h - 1)
                nc.scalar.activation(hTs[p], bank[2 + p][:, 0:256], ACT.Identity, bias=B1).then_inc(h_ev, 1)

            over(act, HALVES - 1, [(0, h_evac)])
            for k, (to, n) in enumerate(((srcT, 0), (relT, 1), (endT, 2))):
                for c in range(0, COLS, 4):
                    w = min(4, COLS - c)
                    act.wait_ge(list_tr, n * COLS + c + w)
                    nc.scalar.copy(to[:, c * ROWS:(c + w) * ROWS], bank[6 + (n * 4 + c // 4) % 2][:, 0:w * ROWS]).then_inc(list_ev, 1)

            def distance(k, g, i):
                act.wait_ge(bc_in[0 if g < 7 else 1], i * 32 + 32)
                after(act, oh_ok, k - 1)
                nc.scalar.activation(SQ[ring(g)], bc[:, 0, g * CH:(g + 1) * CH], ACT.Square, bias=neg_p).then_inc(dist_ok, 1)

            def one_hot(k, g, i):
                act.wait_ge(dist_ok, k + 1)
                after(act, x_mm, k - 1)
                nc.scalar.activation(OH[ring(g)], SQ[ring(g)], ACT.Relu, bias=ones[:, 0:1], scale=-1.0).then_inc(oh_ok, 1)

            def relu(k, g, i):
                act.wait_ge(x_mm, k + 1)
                after(act, v_mm, k - 1)
                nc.scalar.activation(M1[ring(g)], bank[g % 2][:, :], ACT.Relu).then_inc(relu_ok, 1)

            def evac(k, g, i):
                act.wait_ge(s_tr, k + 1)
                after(act, o_mm, k - 1)
                nc.scalar.copy(STs[ring(g)], bank[4 + g % 2][:, :]).then_inc(st_ok, 1)

            groups(act, [(0, distance), (1, relu), (0, one_hot), (4, evac)])

            act.wait_ge(acc_ok, TILES)

            def bias_relu(h, p, w):
                after(act, n1_tr, h - 1)
                settle(act, "act")
                nc.scalar.activation(stg[p][:, :], accT[:, ds(h * 256, 256)], ACT.Relu, bias=B3).then_inc(n1_st, 1)

            over(act, HALVES - 1, [(0, bias_relu)])
            act.wait_ge(stat_ok, 1)
            nc.scalar.activation(tmp[:, :], var[:, :], ACT.Sqrt, bias=eps[:, :]).then_inc(sq_ok, 1)

            def keep(h, p, w):
                act.wait_ge(nm_ok, 2 * h + 2)
                settle(act, "act")
                nc.scalar.copy(X[:, ds(h * 2, 2), 0:F], stg[p][:, :].rearrange("p (b f) -> p b f", b=2)).then_inc(cp_ok, 1)

            def keep_t(h, p, w):
                act.wait_ge(n1_t2, h + 1)
                settle(act, "act")
                nc.scalar.copy(accT[:, ds(h * 256, 256)], bank[2 + p][:, 0:256]).then_inc(x1t_ok, 1)

            def keep_ld(h, p, w):
                act.wait_ge(ld_mm, h + 1)
                after(act, ld_put[p], (h - p) * 8)
                settle(act, "act")
                nc.scalar.activation(lrow[0:1, p, :], bank[4 + p][0:1, 0:256], ACT.Identity, bias=BE[0:1, :]).then_inc(ldb_ok, 1)

            over(act, HALVES - 1, [(0, keep), (0, keep_t), (1, keep_ld)])

            def near_hot(q, s, c):
                i = 2 * q + c
                if c == 0:
                    act.wait_ge(near_in[s], (q - s) * 8 + 16)
                after(act, oh2_ok, i)
                nc.scalar.activation(SQ2, near[:, s, c * HC * T:(c + 1) * HC * T], ACT.Square, bias=neg_p).then_inc(sq2_a, 1)
                act.wait_ge(sq2_a, i + 1)
                after(act, z_ld, (q - 1) * SC + (c + 1) * HC)
                nc.scalar.activation(OH2[c], SQ2, ACT.Relu, bias=ones[:, 0:1], scale=-1.0).then_inc(oh2_ok, 1)

            def spread_windows(q, s):
                act.wait_ge(lw_tr, q + 1)
                after(act, z_ld, (q - 1) * SC)
                nc.scalar.copy(LWd[:, s, 0:SC * SC:SC + 1], bank[7][:, 64:64 + SC]).then_inc(lw_ok, 1)

            def weights(q, s):
                act.wait_ge(z_mm, q + 1)
                after(act, lg_ok, q)
                nc.scalar.mul(low[0:SC, :], bank[4 + s][0:SC, 0:T], SLOPE).then_inc(low_ok, 1)
                act.wait_ge(dif_ok, q + 1)
                after(act, ev_tr, q)
                nc.scalar.activation(exd[0:SC, :], dif[0:SC, :], ACT.Exp).then_inc(exp_ok, 1)
                act.wait_ge(ev_tr, q + 1)
                after(act, sum_ok, (q - 1) * SC)
                after(act, gs_ok, (q - 1) * SC)
                nc.scalar.copy(evr[:, s], bank[7][:, 0:2 * SC].rearrange("p (a t) -> p a t", a=2)).then_inc(ev_ok, 1)

            def scale_rows(q, s, j):
                t = q * SC + j
                u = (s * SC + j) % 4
                if j == 0:
                    act.wait_ge(ev_ok, q + 1)
                after(act, t_mm, t - 3)
                nc.scalar.activation(Gs[u], G[:, s * SC + j, 1:F + 1], ACT.Copy, scale=evr[:, s, 0, j:j + 1]).then_inc(gs_ok, 1)

            def second(i, last=False):
                for s in range(2):
                    q = i * 2 + s
                    more = not (last and s == 1)
                    weights(q, s)
                    for j in range(SC):
                        scale_rows(q, s, j)
                        if more and j == 0:
                            spread_windows(q + 1, 1 - s)
                        if more and j in (1, HC + 1):
                            near_hot(q + 1, 1 - s, j // HC)

            act.wait_ge(cleared, 3)
            spread_windows(0, 0)
            near_hot(0, 0, 0)
            near_hot(0, 0, 1)
            second(0)
            with act.Fori(1, PASSES - 1) as i:
                second(i)
            second(PASSES - 1, last=True)

            def expo(c, p, w):
                act.wait_ge(mm_ok, c + 1)
                after(act, ctx_ok, c - 1)
                nc.scalar.activation(ex[p][:, 0:w], mn[p][:, 0:w], ACT.Exp).then_inc(ex_ok, 1)

            def relu1(c, p, w):
                act.wait_ge(h1_mm, c + 1)
                after(act, h2_mm, c - 1)
                nc.scalar.activation(h1[p][:, 0:w], bank[2 + p][:, 0:w], ACT.Relu, bias=BB1).then_inc(h1_ok, 1)

            def relu2(c, p, w):
                act.wait_ge(h2_mm, c + 1)
                settle(act, "act")
                nc.scalar.activation(H[:, ds(c * CH, w)], bank[4 + p][:, 0:w], ACT.Relu, bias=BB2).then_inc(h2_ok, 1)

            over(act, CHUNKS, [(0, expo), (1, relu1), (2, relu2)], width=CH, tail=N - CHUNKS * CH)
            act.wait_ge(aff_ok, 2)
            nc.scalar.activation(scl[:, :], bnmv[:, 1:2], ACT.Sqrt, bias=eps[:, :]).then_inc(aff_ok, 1)
            act.wait_ge(aff_ok, 7)

            def affine(h, p, w):
                after(act, n2_tr, h - 1)
                settle(act, "act")
                nc.scalar.activation(stg[p][:, :], H[:, ds(h * 256, 256)], ACT.Identity, bias=shf[:, :], scale=scl[:, :]).then_inc(n2_st, 1)

            over(act, HALVES - 1, [(0, affine)])
            act.wait_ge(stat2_ok, 1)
            nc.scalar.activation(tmp[:, :], var[:, :], ACT.Sqrt, bias=eps[:, :]).then_inc(sq2_ok, 1)

        @block.tensor
        def _(pe):
            pe.wait_ge(weights_in, 16 * 18)
            pe.wait_ge(consts, 7)

            def tr_x(h, p, w):
                pe.wait_ge(xin_in[p], (h - p) * 8 + 16)
                after(pe, xt_cp, h - 1)
                for b in range(2):
                    last = nc.tensor.transpose(bank[p][:, b * 128:(b + 1) * 128], xin[p][:, b, :], ident[:, :])
                last.then_inc(xt_tr, 1)

            def mm_h(h, p, w):
                pe.wait_ge(xt_cp, h + 1)
                after(pe, h_ev, h - 1)
                nc.tensor.matmul(bank[2 + p][:, 0:256], W1s[:, :], xTs[p], start=True, stop=True).then_inc(h_mm, 1)

            def mm_pq(h, p, w):
                pe.wait_ge(h_ev, h + 1)
                after(pe, pq_ev, h - 1)
                for b in range(2):
                    last = nc.tensor.matmul(bank[4 + p][:, b * 256:(b + 1) * 256], hTs[p][:, b * 128:(b + 1) * 128],
                                            Wpq[:, :, :].rearrange("k a n -> k (a n)"), start=True, stop=True)
                last.then_inc(pq_mm, 1)

            pe.wait_ge(prep, 1)
            over(pe, HALVES - 1, [(0, tr_x), (1, mm_h), (2, mm_pq)])
            for n, (of, need) in enumerate(((srcF, 2), (rel, 3), (relend, 6))):
                pe.wait_ge(prep, need)
                for c in range(COLS):
                    u = n * 4 + c // 4
                    if c % 4 == 0:
                        after(pe, list_ev, u - 1)
                    nc.tensor.transpose(bank[6 + u % 2][:, c % 4 * ROWS:(c % 4 + 1) * ROWS], of[0:ROWS, c, :],
                                        ident[0:ROWS, 0:ROWS]).then_inc(list_tr, 1)

            def pre(k, g, i):
                pe.wait_ge(landed[g], i * 64 + 64)
                pe.wait_ge(win_in[g], i * 64 + 64)
                pe.wait_ge(oh_ok, k + 1)
                after(pe, relu_ok, used2(k, g))
                for j in range(GT):
                    o = bank[g % 2][:, j * 128:(j + 1) * 128]
                    nc.tensor.matmul(o, G[:, g * GT + j, 0:F], ident[:, :], start=True, stop=False)
                    last = nc.tensor.matmul(o, Pwin[:, g * GT + j, :], OH[ring(g)][:, j * 128:(j + 1) * 128], start=False, stop=True)
                last.then_inc(x_mm, 1)

            def mm3(k, g, i):
                pe.wait_ge(relu_ok, k + 1)
                after(pe, scan_ok, used2(k, g))
                nc.tensor.matmul(bank[2 + g % 2][:, :], W3s[:, :], M1[ring(g)], start=True, stop=True).then_inc(v_mm, 1)

            def tr_s(k, g, i):
                pe.wait_ge(scan_ok, k + 1)
                after(pe, st_ok, used2(k, g))
                for j in range(GT):
                    last = nc.tensor.transpose(bank[4 + g % 2][:, j * 128:(j + 1) * 128], S[ring(g)][:, j * 128:(j + 1) * 128], ident[:, :])
                last.then_inc(s_tr, 1)

            def pick(k, g, i):
                pe.wait_ge(st_ok, k + 1)
                pe.wait_ge(eoh_ok, k + 1)
                after(pe, acc_ok, used2(k, g) * GT)
                for j in range(GT):
                    last = nc.tensor.matmul(bank[6 + g % 2][:, j * 128:(j + 1) * 128], STs[ring(g)][:, j * 128:(j + 1) * 128],
                                            EOH[ring(g)][:, j, :], start=True, stop=True)
                last.then_inc(o_mm, 1)

            groups(pe, [(0, pre), (1, mm3), (3, tr_s), (5, pick)])

            def tr_1(h, p, w):
                pe.wait_ge(n1_st, h + 1)
                after(pe, n1_add, h - 1)
                for b in range(2):
                    last = nc.tensor.transpose(bank[p][:, b * 128:(b + 1) * 128], stg[p][:, b * 128:(b + 1) * 128], ident[:, :])
                last.then_inc(n1_tr, 1)

            over(pe, HALVES - 1, [(0, tr_1)])

            def tr_2(h, p, w):
                pe.wait_ge(nm_ok, 2 * h + 2)
                after(pe, x1t_ok, h - 1)
                for b in range(2):
                    last = nc.tensor.transpose(bank[2 + p][:, b * 128:(b + 1) * 128], stg[p][:, b * 128:(b + 1) * 128], ident[:, :])
                last.then_inc(n1_t2, 1)

            def mm_ld(h, p, w):
                pe.wait_ge(x1t_ok, h + 1)
                after(pe, ldb_ok, h - 1)
                settle(pe, "pe")
                nc.tensor.matmul(bank[4 + p][0:1, 0:256], WDST, accT[:, ds(h * 256, 256)], start=True, stop=True).then_inc(ld_mm, 1)

            over(pe, HALVES - 1, [(0, tr_2), (1, mm_ld)])

            def tr_windows(q, s):
                pe.wait_ge(lw_in[s], (q - s) * (8 * SC) + 16 * SC)
                after(pe, lw_ok, q)
                settle(pe, "pe")
                nc.tensor.transpose(bank[7][:, 64:64 + SC], LW[0:SC, s, :], ident[0:SC, 0:SC]).then_inc(lw_tr, 1)

            def dst_logit(q, s, j):
                if j == 0:
                    pe.wait_ge(lw_ok, q + 1)
                    after(pe, dif_ok, q - 1)
                if j % HC == 0:
                    pe.wait_ge(oh2_ok, 2 * q + j // HC + 1)
                nc.tensor.matmul(bank[4 + s][0:SC, 0:T], LWd[:, s, j * SC:(j + 1) * SC], OH2[j // HC][:, j % HC * T:(j % HC + 1) * T],
                                 start=(j == 0), stop=False).then_inc(z_ld, 1)

            def softmax_mm(i, s):
                q = i * 2 + s
                pe.wait_ge(rows_landed[s], (i + 1) * (16 * SC))
                nc.tensor.matmul(bank[4 + s][0:SC, 0:T], G[:, s * SC:(s + 1) * SC, F + 1], ident[:, :], start=False, stop=True).then_inc(z_mm, 1)
                pe.wait_ge(sc_ok, 3 * q + 1)
                after(pe, run_ok, 2 * q)
                settle(pe, "pe")
                nc.tensor.matmul(bank[6][0:1, 0:SC], fw[0:SC, T - 1:T], ident[0:SC, 0:SC], start=True, stop=True).then_inc(last_tr, 1)
                pe.wait_ge(run_ok, 2 * q + 2)
                after(pe, cr, 3 * q)
                settle(pe, "pe")
                nc.tensor.matmul(bank[6][0:SC, 64:65], run[0:1, s, 0:SC], ones[0:1, 0:1], start=True, stop=True).then_inc(run_tr, 1)
                pe.wait_ge(exp_ok, q + 1)
                after(pe, ev_ok, q)
                settle(pe, "pe")
                nc.tensor.transpose(bank[7][:, 0:SC], exd[0:SC, 0:T], ident[0:SC, 0:SC])
                nc.tensor.matmul(bank[7][:, SC:2 * SC], exd[0:SC, T:T + 1].broadcast_to([SC, 128]), ident[0:SC, 0:SC],
                                 start=True, stop=True).then_inc(ev_tr, 1)

            def sums(q, s, j):
                t = q * SC + j
                u = (s * SC + j) % 4
                pe.wait_ge(gs_ok, t + 1)
                if j % HC == 0:
                    pe.wait_ge(eq_ok, 2 * q + j // HC + 1)
                after(pe, sum_ok, t - 3)
                nc.tensor.matmul(bank[u][:, 0:128], Gs[u], EQ[j // HC][:, j % HC, :], start=True, stop=True).then_inc(t_mm, 1)

            def second(i, last=False):
                for s in range(2):
                    q = i * 2 + s
                    more = not (last and s == 1)
                    softmax_mm(i, s)
                    for j in range(SC):
                        sums(q, s, j)
                        if more and j == 0:
                            tr_windows(q + 1, 1 - s)
                        if more and j >= 3:
                            dst_logit(q + 1, 1 - s, j - 3)
                    for j in range(SC - 3, SC):
                        if more:
                            dst_logit(q + 1, 1 - s, j)

            tr_windows(0, 0)
            for j in range(SC):
                dst_logit(0, 0, j)
            second(0)
            with pe.Fori(1, PASSES - 1) as i:
                second(i)
            second(PASSES - 1, last=True)

            def mm_c(c, p, w):
                after(pe, y_ok, 2 * c - 2)
                nc.tensor.matmul(bank[p][:, 0:w], wprojs[:, :], cacc[:, ds(c * CH, w)], start=True, stop=True)
                nc.tensor.matmul(bank[6 + p][:, 0:w], den_row[:, :], cacc[:, ds(c * CH, w)], start=True, stop=True).then_inc(c_mm, 1)

            def mm_h1(c, p, w):
                pe.wait_ge(ctx_ok, c + 1)
                after(pe, h1_ok, c - 1)
                nc.tensor.matmul(bank[2 + p][:, 0:w], w1s[:, 0, :], ctxb[p][:, 0:w], start=True, stop=False)
                nc.tensor.matmul(bank[2 + p][:, 0:w], w1s[:, 1, :], accT[:, ds(c * CH, w)], start=False, stop=True).then_inc(h1_mm, 1)

            def mm_h2(c, p, w):
                pe.wait_ge(h1_ok, c + 1)
                after(pe, h2_ok, c - 1)
                nc.tensor.matmul(bank[4 + p][:, 0:w], w2s[:, :], h1[p][:, 0:w], start=True, stop=True).then_inc(h2_mm, 1)

            pe.wait_ge(sum_ok, TILES)
            over(pe, CHUNKS, [(0, mm_c), (1, mm_h1), (2, mm_h2)], width=CH, tail=N - CHUNKS * CH)

            def tr_3(h, p, w):
                pe.wait_ge(n2_st, h + 1)
                after(pe, n2_add, h - 1)
                for b in range(2):
                    last = nc.tensor.transpose(bank[p][:, b * 128:(b + 1) * 128], stg[p][:, b * 128:(b + 1) * 128], ident[:, :])
                last.then_inc(n2_tr, 1)

            over(pe, HALVES - 1, [(0, tr_3)])

        @block.vector
        def _(dve):
            v = nc.vector
            done = [0]

            def chain(ins):
                done[0] += 1
                ins.then_inc(turns["dve"], 1)
                dve.wait_ge(turns["dve"], done[0])

            dve.wait_ge(weights_in, 16 * 18)
            dve.wait_ge(consts, 7)
            v.tensor_copy(Wpq[:, 1, :], W2s[:, 1, :])
            v.tensor_tensor(wprojs[0:127, :], wprojs[0:127, :], wproj0[0:127, :], ALU.subtract)
            v.tensor_scalar(den_row[:, :], neg_p.broadcast_to([128, 128]), -127.0, None, ALU.is_equal)
            v.tensor_tensor(Wpq[:, 0, :], W2s[:, 0, :], W2s[:, 1, :], ALU.subtract).then_inc(prep, 1)

            R = slice(0, ROWS)
            here, before, next_ = D[R, :, 1:T + 1], D[R, :, 0:T], D[R, :, 2:T + 2]
            dve.wait_ge(lists_in, 16 * 8)
            v.tensor_copy(srcF[R], S0[R]).then_inc(prep, 1)
            v.tensor_tensor(rel[R], here, D[R, :, 1:2].broadcast_to([ROWS, COLS, T]), ALU.subtract).then_inc(prep, 1)
            chain(v.tensor_tensor(flag[R], here, before, ALU.not_equal))
            dve.wait_ge(prep, 3)
            v.tensor_copy(metaS[R, 0], rel[R])
            v.tensor_scalar(metaS[R, 3], rel[R], 0.0, NEG, ALU.not_equal, ALU.mult)
            chain(v.tensor_scalar(metaS[R, 1], flag[R], NEG, None, ALU.mult))
            chain(v.tensor_scalar(contS[R, :], rel[R, :, T - 1:T].rearrange("p c e -> p (c e)"), 0.0, None, ALU.not_equal))
            v.scalar_tensor_tensor(out=contS[R, :], in0=contS[R, :], scalar=NEG, in1=metaS[R, 1, :, 0:1].rearrange("p c e -> p (c e)"),
                                   op0=ALU.mult, op1=ALU.add).then_inc(prep, 1)
            chain(v.tensor_tensor(flag[R], next_, here, ALU.not_equal))
            v.tensor_scalar(metaS[R, 2], flag[R], NEG, None, ALU.mult).then_inc(prep, 1)
            chain(v.scalar_tensor_tensor(out=relend[R], in0=rel[R], scalar=1.0, in1=flag[R], op0=ALU.add, op1=ALU.mult))
            chain(v.tensor_scalar(relend[R], relend[R], -1.0, None, ALU.add))
            v.engine_nop().then_inc(prep, 2)

            def cp_x(h, p, w):
                dve.wait_ge(xt_tr, h + 1)
                after(dve, h_mm, h - 1)
                v.tensor_copy(xTs[p], bank[p][:, 0:256]).then_inc(xt_cp, 1)

            def ev_pq(h, p, w):
                dve.wait_ge(pq_mm, h + 1)
                after(dve, pq_out[p], (h - p) * 16)
                v.tensor_tensor(pqs[p], bank[4 + p][:, :].rearrange("p (b n) -> p b n", b=2),
                                brow[:, :, :].rearrange("p a n -> p (a n)").unsqueeze(1).broadcast_to([128, 2, 256]), ALU.add).then_inc(pq_ev, 1)

            over(dve, HALVES - 1, [(0, cp_x), (2, ev_pq)])
            dve.wait_ge(list_ev, 12)
            dve.wait_ge(rows_in, 16)
            dve.wait_ge(base_in, 32)
            dve.wait_ge(cleared, 1)

            at = {}

            def scan(k, g, i):
                dve.wait_ge(v_mm, k + 1)
                after(dve, s_tr, k - 1)
                after(dve, scan_ok, k)
                first = isinstance(k, int) and k == 0
                v.tensor_tensor_scan(out=S[ring(g)], data0=bc[:, 1, g * CH:(g + 1) * CH], data1=bank[2 + g % 2][:, :],
                                     initial=NEG if first else S[ring((g - 1) % GROUPS)][:, CH - 1:CH], op0=ALU.add, op1=ALU.max).then_inc(scan_ok, 1)

            def ends(k, g, i):
                after(dve, o_mm, k - 1)
                v.tensor_tensor(EOH[ring(g)], iota_n[:, :].unsqueeze(1).broadcast_to([128, GT, 128]),
                                endT[:, ds(k * GT, GT)].unsqueeze(2).broadcast_to([128, GT, 128]), ALU.is_equal).then_inc(eoh_ok, 1)

            def add_up(j):
                def f(k, g, i):
                    if j == 0:
                        at[0] = bases(mybir.EngineType.DVE, k * GT, GT)
                    win = accT[:, ds(at[0][j], 128)]
                    if j == 0:
                        dve.wait_ge(o_mm, k + 1)
                    after(dve, acc_ok, k * GT + j)
                    v.tensor_tensor(win, win, bank[6 + g % 2][:, j * 128:(j + 1) * 128], ALU.add).then_inc(acc_ok, 1)
                return f

            groups(dve, [(6, add_up(0)), (2, scan), (6, add_up(1)), (4, ends), (6, add_up(2)), (6, add_up(3))])

            def add_to_x(sem_tr, sem_add):
                def f(h, p, w):
                    dve.wait_ge(sem_tr, h + 1)
                    xs = X[:, ds(h * 2, 2), 0:F]
                    v.tensor_tensor(xs, xs, bank[p][:, 0:256].rearrange("p (b f) -> p b f", b=2), ALU.add).then_inc(sem_add, 1)
                return f

            def row_stats(sem_add, sem_bn):
                def f(h, p, w):
                    dve.wait_ge(sem_add, h + 1)
                    settle(dve, "sp")
                    for b in range(2):
                        v.bn_stats(stats[:, ds(h * 2 + b, 1), :].rearrange("p a b -> p (a b)"), X[:, ds(h * 2 + b, 1), 0:F].rearrange("p a b -> p (a b)")).then_inc(sem_bn, 1)
                return f

            def moments(sem_bn, ready):
                dve.wait_ge(sem_bn, BLOCKS)
                me, ve, mo, vo = (stats[:, :, k] for k in (1, 2, 4, 5))
                chain(v.tensor_tensor(tmp[:, :], me, mo, ALU.subtract))
                chain(v.tensor_tensor(mean[:, :], me, mo, ALU.add))
                chain(v.tensor_tensor(var[:, :], ve, vo, ALU.add))
                chain(v.tensor_tensor(tmp[:, :], tmp[:, :], tmp[:, :], ALU.mult))
                chain(v.tensor_scalar(mean[:, :], mean[:, :], 0.5, None, ALU.mult))
                chain(v.tensor_scalar(tmp[:, :], tmp[:, :], 0.25, None, ALU.mult))
                v.scalar_tensor_tensor(out=var[:, :], in0=var[:, :], scalar=1.0 / F, in1=tmp[:, :], op0=ALU.mult, op1=ALU.add).then_inc(ready, 1)

            def scales(sq):
                dve.wait_ge(sq, 1)
                chain(v.reciprocal(rstd[:, :], tmp[:, :]))
                chain(v.scalar_tensor_tensor(out=nmr[:, :], in0=mean[:, :], scalar=-1.0, in1=rstd[:, :], op0=ALU.mult, op1=ALU.mult))

            dve.wait_ge(x_in, 32)
            over(dve, HALVES - 1, [(0, add_to_x(n1_tr, n1_add)), (1, row_stats(n1_add, n1_bn))])
            moments(n1_bn, stat_ok)
            scales(sq_ok)

            def normalise(h, p, w):
                after(dve, cp_ok, h - 1)
                after(dve, n1_t2, h - 1)
                after(dve, ls_ok, 2 * h - 2)
                for b in range(2):
                    v.tensor_scalar(stg[p][:, b * 128:(b + 1) * 128], X[:, ds(h * 2 + b, 1), 0:F].rearrange("p a b -> p (a b)"),
                                    rstd[:, ds(h * 2 + b, 1)], nmr[:, ds(h * 2 + b, 1)], ALU.mult, ALU.add).then_inc(nm_ok, 1)

            def src_logit(h, p, w):
                dve.wait_ge(nm_ok, 2 * h + 2)
                after(dve, ls_ok, 2 * h - 2)
                for b in range(2):
                    v.scalar_tensor_tensor(out=junk[:, 2 * p + b, :], in0=stg[p][:, b * 128:(b + 1) * 128], scalar=1.0, in1=wsrc_row[:, :],
                                           op0=ALU.mult, op1=ALU.mult,
                                           accum_out=X[:, ds(h * 2 + b, 1), F + 1:F + 2].rearrange("p a b -> p (a b)")).then_inc(ls_ok, 1)

            over(dve, HALVES - 1, [(0, normalise), (1, src_logit)])

            def softmax(i, s):
                q = i * 2 + s
                logits = bank[4 + s][0:SC, 0:T]
                starts, finishes, others = (mts[s][0:SC, k, :] for k in range(3))
                dve.wait_ge(low_ok, q + 1)
                after(dve, dif_ok, q)
                v.tensor_tensor(lg[0:SC, :], logits, low[0:SC, :], ALU.max).then_inc(lg_ok, 1)
                dve.wait_ge(lg_ok, q + 1)
                dve.wait_ge(meta_in[s], i * 16 + 16)
                after(dve, last_tr, q)
                v.tensor_tensor_scan(out=fw[0:SC, :], data0=starts, data1=lg[0:SC, :], initial=NEG, op0=ALU.add, op1=ALU.max).then_inc(sc_ok, 1)
                v.tensor_tensor_scan(out=bk[0:SC, ::-1], data0=finishes[:, ::-1], data1=lg[0:SC, ::-1], initial=NEG, op0=ALU.add, op1=ALU.max).then_inc(sc_ok, 1)
                after(dve, run_tr, q - 1)
                v.tensor_copy(run[0:1, s, 0:1], run[0:1, 1 - s, SC:SC + 1]).then_inc(run_ok, 1)
                dve.wait_ge(last_tr, q + 1)
                dve.wait_ge(run_ok, 2 * q + 1)
                v.tensor_tensor_scan(out=run[0:1, s, 1:SC + 1], data0=cont[:, ds(q * SC, SC)], data1=bank[6][0:1, 0:SC],
                                     initial=run[0:1, s, 0:1], op0=ALU.add, op1=ALU.max).then_inc(run_ok, 1)
                dve.wait_ge(sc_ok, 3 * q + 2)
                v.tensor_tensor(mM[0:SC, :], fw[0:SC, :], bk[0:SC, :], ALU.max).then_inc(sc_ok, 1)
                dve.wait_ge(run_tr, q + 1)
                v.tensor_tensor(carry[0:SC, :], bank[6][0:SC, 64:65], starts[:, 0:1], ALU.add).then_inc(cr, 1)
                dve.wait_ge(cr, 3 * q + 1)
                dve.wait_ge(sc_ok, 3 * q + 3)
                v.scalar_tensor_tensor(out=mM[0:SC, :], in0=others, scalar=carry[0:SC, :], in1=mM[0:SC, :], op0=ALU.add, op1=ALU.max).then_inc(cr, 1)
                dve.wait_ge(cr, 3 * q + 2)
                after(dve, exp_ok, q)
                v.tensor_tensor(dif[0:SC, T:T + 1], carry[0:SC, :], mM[0:SC, 0:1], ALU.subtract).then_inc(cr, 1)
                dve.wait_ge(cr, 3 * q + 3)
                v.tensor_tensor(dif[0:SC, 0:T], lg[0:SC, :], mM[0:SC, :], ALU.subtract).then_inc(dif_ok, 1)

            def columns(q, c):
                after(dve, t_mm, (q - 1) * SC + (c + 1) * HC)
                v.tensor_tensor(EQ[c], iota_n[:, :].unsqueeze(1).broadcast_to([128, HC, 128]),
                                relT[:, ds(q * SC + c * HC, HC)].unsqueeze(2).broadcast_to([128, HC, 128]), ALU.is_equal).then_inc(eq_ok, 1)

            def sum_up(q, s, j, at):
                t = q * SC + j
                win = cacc[:, ds(at[j % LD], 128)]
                dve.wait_ge(t_mm, t + 1)
                after(dve, sum_ok, t)
                v.scalar_tensor_tensor(out=win, in0=win, scalar=evr[:, s, 1, j:j + 1], in1=bank[(s * SC + j) % 4][:, 0:128],
                                       op0=ALU.mult, op1=ALU.add).then_inc(sum_ok, 1)

            def second(i):
                for s in range(2):
                    q = i * 2 + s
                    softmax(i, s)
                    columns(q, 0)
                    for j in range(SC):
                        if j % LD == 0:
                            here = bases(mybir.EngineType.DVE, q * SC + j, LD)
                        sum_up(q, s, j, here)
                        if j == 1:
                            columns(q, 1)

            dve.wait_ge(ls_ok, BLOCKS)
            dve.wait_ge(cleared, 2)
            second(0)
            with dve.Fori(1, PASSES) as i:
                second(i)

            def ratio(c, p, w):
                dve.wait_ge(c_mm, c + 1)
                after(dve, mm_ok, c - 1)
                v.reciprocal(rec[p][:, 0:w], bank[6 + p][:, 0:w]).then_inc(y_ok, 1)
                dve.wait_ge(y_ok, 2 * c + 1)
                v.tensor_tensor(Y[p][:, 0:w], bank[p][:, 0:w], rec[p][:, 0:w], ALU.mult).then_inc(y_ok, 1)

            def signs(c, p, w):
                dve.wait_ge(y_ok, 2 * c + 2)
                after(dve, ctx_ok, c - 1)
                v.tensor_scalar(mx[p][:, 0:w], Y[p][:, 0:w], 0.0, None, ALU.max)
                v.tensor_scalar(mn[p][:, 0:w], Y[p][:, 0:w], 0.0, None, ALU.min).then_inc(mm_ok, 1)

            def elu(c, p, w):
                dve.wait_ge(ex_ok, c + 1)
                dve.wait_ge(mm_ok, c + 1)
                after(dve, h1_mm, c - 1)
                v.scalar_tensor_tensor(out=ctxb[p][:, 0:w], in0=ex[p][:, 0:w], scalar=-1.0, in1=mx[p][:, 0:w], op0=ALU.add, op1=ALU.add).then_inc(ctx_ok, 1)

            def col_stats(c, p, w):
                dve.wait_ge(h2_ok, c + 1)
                settle(dve, "sp")
                v.bn_stats(bnst[:, ds(c, 1), :].rearrange("p a b -> p (a b)"), H[:, ds(c * CH, w)]).then_inc(bn_ok, 1)

            dve.wait_ge(sum_ok, TILES)
            over(dve, CHUNKS, [(0, ratio), (0, signs), (1, elu), (3, col_stats)], width=CH, tail=N - CHUNKS * CH)
            dve.wait_ge(bn_ok, CHUNKS + 1)
            v.bn_aggr(bnmv[:, :], bnst[:, :, :].rearrange("p a b -> p (a b)")).then_inc(aff_ok, 2)
            dve.wait_ge(aff_ok, 3)
            v.reciprocal(scl[:, :], scl[:, :]).then_inc(aff_ok, 1)
            dve.wait_ge(aff_ok, 4)
            v.tensor_tensor(scl[:, :], scl[:, :], GAM, ALU.mult).then_inc(aff_ok, 1)
            dve.wait_ge(aff_ok, 5)
            v.scalar_tensor_tensor(out=shf[:, :], in0=bnmv[:, 0:1], scalar=-1.0, in1=scl[:, :], op0=ALU.mult, op1=ALU.mult).then_inc(aff_ok, 1)
            dve.wait_ge(aff_ok, 6)
            v.tensor_tensor(shf[:, :], shf[:, :], BET, ALU.add).then_inc(aff_ok, 1)

            over(dve, HALVES - 1, [(0, add_to_x(n2_tr, n2_add)), (1, row_stats(n2_add, n2_bn))])
            moments(n2_bn, stat2_ok)
            scales(sq2_ok)

            def finish(h, p, w):
                after(dve, out_done[p], (h - p) * 8)
                for b in range(2):
                    v.tensor_scalar(outs[p][:, b, :], X[:, ds(h * 2 + b, 1), 0:F].rearrange("p a b -> p (a b)"),
                                    rstd[:, ds(h * 2 + b, 1)], nmr[:, ds(h * 2 + b, 1)], ALU.mult, ALU.add).then_inc(nm2_ok, 1)

            over(dve, HALVES - 1, [(0, finish)])


_INS = ['x', 'src', 'dst', 'L0_gnn_W1', 'L0_gnn_b1', 'L0_gnn_W2', 'L0_gnn_b2', 'L0_gnn_W3', 'L0_gnn_b3',
        'L1_gnn_we_dst', 'L1_gnn_we_src', 'L1_gnn_be', 'L1_gnn_w_proj', 'L1_gnn_b_proj', 'L1_gnn_w1', 'L1_gnn_b1',
        'L1_gnn_w2', 'L1_gnn_b2', 'L1_gnn_gamma', 'L1_gnn_beta']


def kernel(**inputs):
    import numpy as _np
    import concourse.bacc as _bacc
    from concourse import mybir as _mybir
    from concourse.bass_utils import run_bass_kernel_spmd as _run

    nc = _bacc.Bacc("TRN2", target_bir_lowering=False, num_devices=1)
    arrays, args = {}, []
    for name in _INS:
        a = _np.ascontiguousarray(inputs[name])
        arrays[f"in_{name}"] = a
        args.append(nc.dram_tensor(f"in_{name}", a.shape, _mybir.dt.from_np(a.dtype), kind="ExternalInput").ap())
    args.append(nc.dram_tensor("out_0", (N, F), _mybir.dt.float32, kind="ExternalOutput").ap())
    build(nc, *args)
    r = _run(nc, [arrays], core_ids=[0])
    return r.results[0]["out_0"]
```

```python
import concourse.bass as bass
from concourse import mybir
from contextlib import ExitStack

N = 6250
E = 206250
F = 128
T = 128
TILES = -(-E // T)
PASS = 52
PASSES = TILES // PASS
GT = 4
GROUPS = PASS // GT
SC = PASS // 2
HC = SC // 2
LD = HC
ROWS = 124
COLS = TILES // ROWS
CH = 512
CHUNKS = N // CH
SB = CH // 128
STEPS = CHUNKS + 1
BLOCKS = SB * STEPS
NP = BLOCKS * 128
LP, LR = divmod(N - CHUNKS * CH, SB)
EVEN, ODD = (STEPS + 1) // 2, STEPS // 2
RP = 125
TAB = 132
EPS = 1e-5
SLOPE = 0.01
NEG = -1.0e38
assert TILES == PASS * PASSES == ROWS * COLS and PASS == GT * GROUPS
assert CHUNKS % 2 == 0 and LP > 0 and LR > 0 and N % RP == 0


def build(nc, x, src, dst, W1, b1, W2, b2, W3, b3, we_dst, we_src, be, w_proj, b_proj,
          w1, bb1, w2, bb2, gamma, beta, out):
    fp32, bf16, i32 = mybir.dt.float32, mybir.dt.bfloat16, mybir.dt.int32
    ALU, ACT = mybir.AluOpType, mybir.ActivationFunctionType
    ds = bass.ds
    nc.disable_value_cache = True

    p_tab = nc.dram_tensor("p_tab", (NP, F), fp32, kind="Internal").ap()
    q_tab = nc.dram_tensor("q_tab", (NP, F), fp32, kind="Internal").ap()
    x1_tab = nc.dram_tensor("x1_tab", (NP, TAB), fp32, kind="Internal").ap()
    meta = nc.dram_tensor("meta", (4, TILES * T), bf16, kind="Internal").ap()
    ld_d = nc.dram_tensor("ld_d", (1, NP), fp32, kind="Internal").ap()
    den_d = nc.dram_tensor("den_d", (1, N), fp32, kind="Internal").ap()
    inv_d = nc.dram_tensor("inv_d", (1, N), fp32, kind="Internal").ap()
    cont_d = nc.dram_tensor("cont_d", (1, TILES), fp32, kind="Internal").ap()

    ctx = ExitStack()
    with ctx:
        def sb(name, shape, dt=fp32):
            return ctx.enter_context(nc.sbuf_tensor(name, shape, dt))

        def sem(name):
            return ctx.enter_context(nc.semaphore(name))

        ident, iota_n, ones = sb("ident", [128, 128]), sb("iota_n", [128, 128]), sb("ones", [128, 128])
        W1s, W2s, Wpq, W3s = sb("W1s", [128, 128]), sb("W2s", [128, 2, 128]), sb("Wpq", [128, 2, 128]), sb("W3s", [128, 128])
        wprojs, w1s, w2s = sb("wprojs", [128, 128]), sb("w1s", [128, 2, 128]), sb("w2s", [128, 128])
        brow = sb("brow", [128, 2, 128])
        wsrc_row = sb("wsrc_row", [128, 128])
        wproj0 = sb("wproj0", [128, 128])
        cols = sb("cols", [128, 9])
        B1, B3, BB1, BB2, GAM, BET, WDST, BE, neg_p = (cols[:, i:i + 1] for i in range(9))
        srcT, relT, endT = sb("srcT", [128, TILES], i32), sb("relT", [128, TILES]), sb("endT", [128, TILES])
        rows = sb("rows", [128, TILES])
        cont = rows[0:1, :]
        base = rows[64:65, :].bitcast(i32)
        idx = sb("idx", [128, PASS], i32)
        X = sb("X", [128, BLOCKS, TAB])
        accT = sb("accT", [128, NP])
        G = sb("G", [128, PASS, TAB])
        ZW = 21760
        Z = sb("Z", [128, ZW])
        stats = sb("stats", [128, BLOCKS, 6])
        mean, var, rstd, nmr, tmp = (sb(n, [128, BLOCKS]) for n in ("mean", "var", "rstd", "nmr", "tmp"))
        bnst, bnmv = sb("bnst", [128, CHUNKS + 1, 6]), sb("bnmv", [128, 2])
        scl, shf, eps = sb("scl", [128, 1]), sb("shf", [128, 1]), sb("eps", [128, 1])

        top = [0]

        def z(shape, dt=fp32):
            n = 1
            for s in shape:
                n *= s
            words = n if dt != bf16 else n // 2
            assert top[0] + words <= ZW
            part = Z[:, top[0]:top[0] + words]
            top[0] += words
            assert top[0] <= ZW, top[0]
            if dt != fp32:
                part = part.bitcast(dt)
            if len(shape) == 2:
                part = part.rearrange("p (a b) -> p a b", a=shape[0])
            if len(shape) == 3:
                part = part.rearrange("p (a b c) -> p a b c", a=shape[0], b=shape[1])
            return part

        D = z([COLS, T + 2], i32)
        S0 = z([COLS, T], i32)
        srcF, rel, relend, flag = z([COLS, T]), z([COLS, T]), z([COLS, T]), z([COLS, T])
        metaS = z([4, COLS, T], bf16)
        contS = z([COLS])
        xTs = [z([CH]) for _ in range(2)]
        hTs = [z([CH]) for _ in range(2)]
        pqs = [z([SB, 256]) for _ in range(2)]
        top[0] = 0
        Pwin = z([PASS, 128])
        bc = z([2, PASS * T], bf16)
        SQ = [z([CH], bf16) for _ in range(3)]
        OH = [z([CH]) for _ in range(3)]
        M1 = [z([CH]) for _ in range(3)]
        S = [z([CH]) for _ in range(3)]
        STs = [z([CH]) for _ in range(3)]
        EOH = [z([GT, 128]) for _ in range(3)]
        top[0] = 0
        cacc = z([NP])
        H = cacc
        z2 = top[0]
        near = z([2, SC * T], bf16)
        SQ2 = z([HC * T], bf16)
        OH2 = [z([HC * T]) for _ in range(2)]
        EQ = [z([HC, 128]) for _ in range(2)]
        LWd = z([2, SC * SC])
        Gs = [z([128]) for _ in range(4)]
        LW = z([2, 128])
        mts = [z([3, T], bf16) for _ in range(2)]
        fw, bk, mM, low, lg = (z([T]) for _ in range(5))
        dif, exd = z([T + 1]), z([T + 1])
        top[0] = z2
        rec, Y, mn, mx, ex, ctxb, h1 = ([z([CH]) for _ in range(2)] for _ in range(7))
        outs = [z([SB, 128]) for _ in range(2)]
        inv = z([N])[0:1, :]
        dens = sb("dens", [128, N // RP])
        stg = [sb(f"stg{i}", [128, CH]) for i in range(2)]
        lrow = [EQ[p].rearrange("p a b -> p (a b)")[0:1, 0:CH] for p in range(2)]
        lprod = [EQ[p][:, SB:2 * SB, :] for p in range(2)]
        nrm = [OH2[p].rearrange("p (a b) -> p a b", a=HC)[:, 0:SB, :] for p in range(2)]
        run = sb("run", [128, 2, SC + 1])
        carry = sb("carry", [128, 1])
        evr = sb("evr", [128, 2, 2, SC])

        bank = [ctx.enter_context(nc.psum_tensor(f"bank{i}", [128, 512], fp32)) for i in range(8)]

        weights_in, x_in, lists_in, base_in, rows_in = (sem(n) for n in ("weights_in", "x_in", "lists_in", "base_in", "rows_in"))
        consts, pads, prep = sem("consts"), sem("pads"), sem("prep")
        x_st = [sem(f"x_st{i}") for i in range(2)]
        xt_tr, xt_cp, h_mm, h_ev, pq_mm, pq_ev = (sem(n) for n in ("xt_tr", "xt_cp", "h_mm", "h_ev", "pq_mm", "pq_ev"))
        pq_out = [sem(f"pq_out{i}") for i in range(2)]
        meta_out, cont_out, list_tr, list_ev = sem("meta_out"), sem("cont_out"), sem("list_tr"), sem("list_ev")
        idx_ok = sem("idx_ok")
        landed = [sem(f"landed{g}") for g in range(GROUPS)]
        win_in = [sem(f"win_in{g}") for g in range(GROUPS)]
        bc_in = [sem(f"bc_in{i}") for i in range(2)]
        dist_ok, oh_ok, x_mm, relu_ok, v_mm, scan_ok, s_tr, st_ok, eoh_ok, o_mm, acc_ok = (sem(n) for n in (
            "dist_ok", "oh_ok", "x_mm", "relu_ok", "v_mm", "scan_ok", "s_tr", "st_ok", "eoh_ok", "o_mm", "acc_ok"))
        n1_st, n1_tr, n1_add, n1_bn, stat_ok, sq_ok = (sem(n) for n in ("n1_st", "n1_tr", "n1_add", "n1_bn", "stat_ok", "sq_ok"))
        sc1_ok, nm_ok, lp_ok, ls_ok, cp_ok, n1_t2, x1t_ok, ld_mm, ldb_ok, tab_out = (sem(n) for n in (
            "sc1_ok", "nm_ok", "lp_ok", "ls_ok", "cp_ok", "n1_t2", "x1t_ok", "ld_mm", "ldb_ok", "tab_out"))
        cleared = sem("cleared")
        meta_in = [sem(f"meta_in{i}") for i in range(2)]
        rows_landed = [sem(f"rows_landed{i}") for i in range(2)]
        ld_put, lw_tr, lw_ok, near_in, lw_in = [sem(f"ld_put{i}") for i in range(2)], sem("lw_tr"), sem("lw_ok"), [sem(f"near_in{i}") for i in range(2)], [sem(f"lw_in{i}") for i in range(2)]
        sq2_a, oh2_ok, z_ld, z_mm, low_ok, lg_ok, sc_ok, last_tr, run_ok, run_tr, cr, dif_ok, exp_ok, ev_tr, ev_ok = (sem(n) for n in (
            "sq2_a", "oh2_ok", "z_ld", "z_mm", "low_ok", "lg_ok", "sc_ok", "last_tr", "run_ok", "run_tr", "cr", "dif_ok", "exp_ok", "ev_tr", "ev_ok"))
        eq_ok, gs_ok, t_mm, sum_ok = sem("eq_ok"), sem("gs_ok"), sem("t_mm"), sem("sum_ok")
        y_ok, c_mm, mm_ok, ex_ok, ctx_ok, h1_mm, h1_ok, h2_mm, h2_ok, bn_ok = (sem(n) for n in (
            "y_ok", "c_mm", "mm_ok", "ex_ok", "ctx_ok", "h1_mm", "h1_ok", "h2_mm", "h2_ok", "bn_ok"))
        aff_ok, n2_st, n2_tr, n2_add, n2_bn, stat2_ok, sq2_ok, sc2_ok, nm2_ok = (sem(n) for n in (
            "aff_ok", "n2_st", "n2_tr", "n2_add", "n2_bn", "stat2_ok", "sq2_ok", "sc2_ok", "nm2_ok"))
        den_out, den_in, inv_ok, inv_out, inv_in, rec_ok = (sem(n) for n in ("den_out", "den_in", "inv_ok", "inv_out", "inv_in", "rec_ok"))
        out_done = [sem(f"out_done{i}") for i in range(2)]
        turns = {e: sem(f"turns_{e}") for e in ("pool", "act", "dve", "dve_waits", "pe", "sp")}

        def after(eng, s, n):
            if not isinstance(n, int) or n > 0:
                eng.wait_ge(s, n)

        def settle(eng, name):
            eng.sem_inc(turns[name], 1)

        def over(eng, full, stages, width=None, tail=None):
            lag = max(k for k, _ in stages)
            first = 4

            def step(h, p, static):
                for k, f in stages:
                    if static and not 0 <= h - k <= full:
                        continue
                    f(h - k, (p - k) % 2, tail if static and h - k == full else width)

            for h in range(first):
                step(h, h % 2, True)
            assert lag <= first and full % 2 == 0
            with eng.Fori(first // 2, full // 2) as i:
                step(i * 2, 0, False)
                step(i * 2 + 1, 1, False)
            for h in range(full, full + 1 + lag):
                step(h, h % 2, True)

        def groups(eng, stages):
            def a_pass(i, upto=GROUPS):
                for g in range(upto):
                    for k, f in stages:
                        gg, ii = (g - k, i) if g >= k else (g - k + GROUPS, i - 1)
                        if isinstance(i, int) and (ii < 0 or ii >= PASSES):
                            continue
                        f(ii * GROUPS + gg, gg, ii)

            a_pass(0)
            with eng.Fori(1, PASSES) as i:
                a_pass(i)
            a_pass(PASSES, max(k for k, _ in stages))

        def bases(engine, t, n):
            _, got = nc.values_load_multi_w_load_instructions(base[0:1, ds(t, n)], engines=(engine,), min_val=0, max_val=NP - 128,
                                                             skip_runtime_bounds_check_because="a destination is a node, so below N")
            return got

        def step_of(h):
            return X[:, ds(h * SB, SB), 0:F]

        def block_of(h, b):
            return X[:, ds(h * SB + b, 1), 0:F].rearrange("p a b -> p (a b)")

        def in_order(a):
            return a.rearrange("f (q b) -> f q b", b=SB)

        def by_block(a):
            return a.rearrange("f (b q) -> f q b", b=SB)

        def used2(k, g):
            return k if g == 0 else k - 1

        def ring(g):
            return 2 if g == GROUPS - 1 else g % 2

        def stage(eng, unit, parity):
            def f(h, p, w):
                if p == parity:
                    after(eng, xt_tr, h - 1)
                    settle(eng, ("pool", "dve_waits")[parity])
                    unit.tensor_copy(stg[p][:, :].rearrange("p (b f) -> p b f", b=SB), step_of(h)).then_inc(x_st[p], 2)
            return f

        block = ctx.enter_context(nc.Block())

        @block.sync
        def _(sp):
            for h in range(CHUNKS):
                sp.dma_start(X[:, h * SB:(h + 1) * SB, 0:F], x[h * CH:(h + 1) * CH, :].rearrange("(p b) f -> p b f", b=SB)).then_inc(x_in, 16)
            sp.wait_ge(pads, 5)
            sp.dma_start(X[0:LP, SB * CHUNKS:BLOCKS, 0:F], x[CHUNKS * CH:N - LR, :].rearrange("(p b) f -> p b f", b=SB)).then_inc(x_in, 16)
            sp.dma_start(X[LP:LP + 1, SB * CHUNKS:SB * CHUNKS + LR, 0:F], x[N - LR:N, :].rearrange("(p b) f -> p b f", b=LR)).then_inc(x_in, 16)

            with nc.allow_non_contiguous_dma(reason="one number for each tile"):
                sp.dma_start(base[:, 0:TILES - 1], dst[0:(TILES - 1) * T].rearrange("(t e) -> e t", e=T)[0:1, :]).then_inc(base_in, 16)
                sp.dma_start(base[:, TILES - 1:TILES], dst[(TILES - 1) * T:(TILES - 1) * T + 1].rearrange("(a n) -> a n", a=1)).then_inc(base_in, 16)

            def store_pq(h, p, w):
                sp.wait_ge(pq_ev, 2 * h + 2)
                settle(sp, "sp")
                for tab, o in ((p_tab, 0), (q_tab, 128)):
                    sp.dma_start(tab[ds(h * CH, CH), :].rearrange("(p b) f -> p b f", b=SB),
                                 pqs[p][:, :, o:o + 128]).then_inc(pq_out[p], 16)

            over(sp, CHUNKS, [(0, store_pq)])

            sp.wait_ge(prep, 7)
            for k in range(4):
                sp.dma_start(meta[k, :].rearrange("(c p e) -> p c e", p=ROWS, e=T), metaS[0:ROWS, k]).then_inc(meta_out, 16)
            with nc.allow_non_contiguous_dma(reason="one number for each tile"):
                sp.dma_start(cont_d[0, :].rearrange("(c p) -> p c", p=ROWS), contS[0:ROWS, :]).then_inc(cont_out, 16)
            sp.wait_ge(cont_out, 16)
            sp.dma_start(cont, cont_d[:, :]).then_inc(rows_in, 16)
            sp.wait_ge(meta_out, 64)
            sp.wait_ge(base_in, 32)
            sp.wait_ge(pq_out[0], 32 * EVEN)
            sp.wait_ge(pq_out[1], 32 * ODD)
            sp.wait_ge(cont_out, 16)
            sp.wait_ge(list_tr, 3 * COLS)

            def windows(i, g):
                at = bases(mybir.EngineType.SP, i * PASS + g * GT, GT)
                after(sp, x_mm, (i - 1) * GROUPS + g + 1)
                settle(sp, "sp")
                for j in range(GT):
                    sp.dma_start(Pwin[:, g * GT + j, :], p_tab[ds(at[j], 128), :]).then_inc(win_in[g], 16)

            def spread(i, half):
                a, b = ((0, 7), (7, GROUPS))[half]
                after(sp, scan_ok, (i - 1) * GROUPS + b)
                after(sp, dist_ok, (i - 1) * GROUPS + b)
                settle(sp, "sp")
                for k in range(2):
                    sp.dma_start(bc[:, k, a * CH:b * CH],
                                 meta[k:k + 1, ds(i * (PASS * T) + a * CH, (b - a) * CH)].broadcast_to([128, (b - a) * CH])).then_inc(bc_in[half], 16)

            def first_layer(i):
                spread(i, 0)
                for g in range(7):
                    windows(i, g)
                spread(i, 1)
                for g in range(7, GROUPS):
                    windows(i, g)

            first_layer(0)
            with sp.Fori(1, PASSES) as i:
                first_layer(i)

            def store_tab(h, p, w):
                sp.wait_ge(cp_ok, h + 1)
                sp.wait_ge(ls_ok, h + 1)
                settle(sp, "sp")
                sp.dma_start(x1_tab[ds(h * CH, CH), :].rearrange("(p b) f -> p b f", b=SB), X[:, ds(h * SB, SB), :]).then_inc(tab_out, 16)

            def store_ld(h, p, w):
                sp.wait_ge(ldb_ok, h + 1)
                settle(sp, "sp")
                sp.dma_start(ld_d[:, ds(h * CH, CH)], lrow[p]).then_inc(ld_put[p], 16)

            over(sp, CHUNKS, [(0, store_tab), (1, store_ld)])

            sp.wait_ge(ld_put[0], 16 * EVEN)
            sp.wait_ge(ld_put[1], 16 * ODD)

            def load_group(i, s):
                q = i * 2 + s
                after(sp, dif_ok, q - 1)
                settle(sp, "sp")
                after(sp, sq2_a, 2 * (q - 1))
                settle(sp, "sp")
                after(sp, lw_tr, q - 1)
                settle(sp, "sp")
                sp.dma_start(mts[s][0:SC], meta[1:4, ds(q * (SC * T), SC * T)].rearrange("k (t e) -> t k e", e=T)).then_inc(meta_in[s], 16)
                sp.dma_start(near[:, s, :], meta[0:1, ds(q * (SC * T), SC * T)].broadcast_to([128, SC * T])).then_inc(near_in[s], 16)
                for c in range(2):
                    at = bases(mybir.EngineType.SP, q * SC + c * HC, HC)
                    for j in range(HC):
                        sp.dma_start(LW[c * HC + j:c * HC + j + 1, s, :], ld_d[0:1, ds(at[j], 128)]).then_inc(lw_in[s], 16)

            for s in range(2):
                load_group(0, s)
            with sp.Fori(1, PASSES) as i:
                for s in range(2):
                    load_group(i, s)

            sp.wait_ge(sum_ok, TILES)
            sp.dma_start(den_d[:, :], cacc[127:128, 0:N]).then_inc(den_out, 16)
            sp.wait_ge(den_out, 16)
            sp.dma_start(dens[0:RP, :], den_d[0, :].rearrange("(p c) -> p c", p=RP)).then_inc(den_in, 16)
            sp.wait_ge(inv_ok, 1)
            sp.dma_start(inv_d[0, :].rearrange("(p c) -> p c", p=RP), dens[0:RP, :]).then_inc(inv_out, 16)
            sp.wait_ge(inv_out, 16)
            sp.dma_start(inv, inv_d[:, :]).then_inc(inv_in, 16)

            def store_out(h, p, w):
                sp.wait_ge(nm2_ok, h + 1)
                settle(sp, "sp")
                if w:
                    sp.dma_start(out[CHUNKS * CH:N - LR, :].rearrange("(p b) f -> p b f", b=SB), outs[p][0:LP]).then_inc(out_done[p], 16)
                    sp.dma_start(out[N - LR:N, :].rearrange("(p b) f -> p b f", b=LR), outs[p][LP:LP + 1, 0:LR, :]).then_inc(out_done[p], 16)
                else:
                    sp.dma_start(out[ds(h * CH, CH), :].rearrange("(p b) f -> p b f", b=SB), outs[p]).then_inc(out_done[p], 16)

            over(sp, CHUNKS, [(0, store_out)], tail=1)
            sp.wait_ge(out_done[0], 16 * (EVEN + 1))
            sp.wait_ge(out_done[1], 16 * ODD)

        @block.gpsimd
        def _(pool):
            nc.gpsimd.memset(ident[:, :], 0.0).then_inc(turns["pool"], 1)
            nc.gpsimd.memset(D[:, :, :], -1).then_inc(pads, 1)
            nc.gpsimd.memset(S0[:, :, :], 0).then_inc(pads, 1)
            nc.gpsimd.memset(X[:, SB * CHUNKS:BLOCKS, 0:F], 0.0).then_inc(pads, 1)
            nc.gpsimd.memset(X[:, :, F + 1:TAB], 0.0).then_inc(pads, 1)
            nc.gpsimd.memset(X[:, :, F:F + 1], 1.0).then_inc(pads, 1)
            nc.gpsimd.iota(iota_n[:, :], pattern=[[1, 128]], base=0, channel_multiplier=0, allow_small_or_imprecise_dtypes=True).then_inc(consts, 1)
            nc.gpsimd.iota(neg_p, pattern=[[0, 1]], base=0, channel_multiplier=-1, allow_small_or_imprecise_dtypes=True).then_inc(consts, 1)
            nc.gpsimd.memset(ones[:, :], 1.0).then_inc(consts, 1)
            nc.gpsimd.memset(eps[:, :], EPS).then_inc(consts, 1)
            nc.gpsimd.memset(run[:, :, :], NEG).then_inc(consts, 1)
            nc.gpsimd.memset(brow[:, 1, :], 0.0).then_inc(consts, 1)
            pool.wait_ge(turns["pool"], 1)
            nc.gpsimd.affine_select(out=ident[:, :], in_=ident[:, :], compare_op=ALU.not_equal, fill=1.0, base=0,
                                    pattern=[[-1, 128]], channel_multiplier=1).then_inc(consts, 1)
            pool.wait_ge(pads, 2)
            whole = ROWS * T
            end = (COLS - 1) * whole
            pool.dma_start(D[0:1, 0, 1:T + 2], dst[0:T + 1].rearrange("(a n) -> a n", a=1)).then_inc(lists_in, 16)
            pool.dma_start(D[1:ROWS, 0, 0:T + 2], bass.AP(dst.tensor, T - 1, [[T, ROWS - 1], [1, T + 2]])).then_inc(lists_in, 16)
            pool.dma_start(D[0:ROWS, 1:COLS - 1, 0:T + 2], bass.AP(dst.tensor, whole - 1, [[T, ROWS], [whole, COLS - 2], [1, T + 2]])).then_inc(lists_in, 16)
            pool.dma_start(D[0:ROWS - 1, COLS - 1, 0:T + 2], bass.AP(dst.tensor, end - 1, [[T, ROWS - 1], [1, T + 2]])).then_inc(lists_in, 16)
            pool.dma_start(D[ROWS - 1:ROWS, COLS - 1, 0:E - (TILES - 1) * T + 1], dst[(TILES - 1) * T - 1:E].rearrange("(a n) -> a n", a=1)).then_inc(lists_in, 16)
            pool.dma_start(S0[0:ROWS, 0:COLS - 1, :], src[0:end].rearrange("(c p e) -> p c e", p=ROWS, e=T)).then_inc(lists_in, 16)
            pool.dma_start(S0[0:ROWS - 1, COLS - 1, :], src[end:(TILES - 1) * T].rearrange("(p e) -> p e", e=T)).then_inc(lists_in, 16)
            pool.dma_start(S0[ROWS - 1:ROWS, COLS - 1, 0:E - (TILES - 1) * T], src[(TILES - 1) * T:E].rearrange("(a n) -> a n", a=1)).then_inc(lists_in, 16)
            nc.gpsimd.memset(accT[:, :], 0.0).then_inc(cleared, 1)

            half = PASS // 2

            def indices(i, s, free):
                for f, n in free:
                    after(pool, f, n)
                settle(pool, "pool")
                nc.gpsimd.tensor_copy(idx[:, s * half:(s + 1) * half], srcT[:, ds(i * PASS + s * half, half)]).then_inc(idx_ok, 1)

            pool.wait_ge(x_in, 16 * (STEPS + 1))
            over(pool, CHUNKS, [(0, stage(pool, nc.gpsimd, 0))])

            pool.wait_ge(list_ev, 4)
            pool.wait_ge(pq_out[0], 32 * EVEN)
            pool.wait_ge(pq_out[1], 32 * ODD)

            def gather_q(i):
                indices(i, 0, [(landed[g], i * 64) for g in range(7)])
                pool.wait_ge(idx_ok, i * 2 + 1)
                for g in range(GROUPS):
                    if g == 6:
                        indices(i, 1, [(landed[u], i * 64) for u in range(7, GROUPS)] + [(landed[6], i * 64)])
                        pool.wait_ge(idx_ok, i * 2 + 2)
                    after(pool, x_mm, (i - 1) * GROUPS + g + 1)
                    settle(pool, "pool")
                    for j in range(g * GT, g * GT + GT):
                        pool.indirect_dma_start(G[:, j, 0:F], None, q_tab[:, :],
                                                bass.IndirectOffsetOnAxis(ap=idx[:, j:j + 1], axis=0)).then_inc(landed[g], 16)

            gather_q(0)
            with pool.Fori(1, PASSES) as i:
                gather_q(i)

            pool.wait_ge(acc_ok, TILES)
            nc.gpsimd.memset(cacc, 0.0).then_inc(cleared, 1)
            nc.gpsimd.memset(LWd, 0.0).then_inc(cleared, 1)

            def src_product(h, p, w):
                pool.wait_ge(nm_ok, h + 1)
                settle(pool, "pool")
                after(pool, ls_ok, h - 1)
                settle(pool, "pool")
                nc.gpsimd.tensor_tensor(lprod[p], nrm[p], wsrc_row[:, :].unsqueeze(1).broadcast_to([128, SB, F]), ALU.mult).then_inc(lp_ok, 1)

            pool.wait_ge(weights_in, 16 * 18)
            over(pool, CHUNKS, [(0, src_product)])
            for g in range(GROUPS):
                pool.wait_ge(landed[g], 64 * PASSES)
            pool.wait_ge(tab_out, 16 * STEPS)

            def gather_x1(i):
                for s in range(2):
                    indices(i, s, [(rows_landed[s], i * (16 * SC))])
                    pool.wait_ge(idx_ok, (i + PASSES) * 2 + s + 1)
                    for j in range(SC):
                        if j % HC == 0:
                            after(pool, gs_ok, (i - 1) * PASS + s * SC + j + HC)
                            after(pool, z_mm, i * 2 + s - 1)
                            settle(pool, "pool")
                        u = s * SC + j
                        pool.indirect_dma_start(G[:, u, :], None, x1_tab[:, :],
                                                bass.IndirectOffsetOnAxis(ap=idx[:, u:u + 1], axis=0)).then_inc(rows_landed[s], 16)

            gather_x1(0)
            with pool.Fori(1, PASSES) as i:
                gather_x1(i)

        @block.scalar
        def _(act):
            for to, of in ((W1s[:, :], W1[:, :]), (W2s[:, :, :], W2.rearrange("(a k) n -> k a n", a=2)),
                           (W3s[:, :], W3[:, :]), (wprojs[0:127, :], w_proj[1:128, :]),
                           (wprojs[127:128, :], b_proj.rearrange("(a n) -> a n", a=1)), (wproj0[:, :], w_proj[0:1, :].broadcast_to([128, 128])),
                           (w1s[:, :, :], w1.rearrange("(a k) n -> k a n", a=2)), (w2s[:, :], w2[:, :]),
                           (brow[:, 0, :], b2.rearrange("(a n) -> a n", a=1).broadcast_to([128, 128])),
                           (wsrc_row[:, :], we_src.rearrange("(a n) -> a n", a=1).broadcast_to([128, 128]))):
                act.dma_start(to, of).then_inc(weights_in, 16)
            with nc.allow_non_contiguous_dma(reason="a few vectors"):
                for to, of in ((B1, b1), (B3, b3), (BB1, bb1), (BB2, bb2), (GAM, gamma),
                               (BET, beta), (WDST, we_dst)):
                    act.dma_start(to, of.rearrange("(n a) -> n a", a=1)).then_inc(weights_in, 16)
                act.dma_start(BE, be.rearrange("(n a) -> n a", a=1).broadcast_to([128, 1])).then_inc(weights_in, 16)
            act.wait_ge(weights_in, 16 * 18)
            act.wait_ge(consts, 7)

            def x_evac(h, p, w):
                act.wait_ge(xt_tr, h + 1)
                after(act, h_mm, h - 1)
                nc.scalar.copy(xTs[p], bank[p][:, :]).then_inc(xt_cp, 1)

            def h_evac(h, p, w):
                act.wait_ge(h_mm, h + 1)
                after(act, pq_mm, h - 1)
                nc.scalar.activation(hTs[p], bank[2 + p][:, :], ACT.Identity, bias=B1).then_inc(h_ev, 1)

            def keep_list(to, n):
                for c in range(0, COLS, 4):
                    w = min(4, COLS - c)
                    act.wait_ge(list_tr, n * COLS + c + w)
                    nc.scalar.copy(to[:, c * ROWS:(c + w) * ROWS], bank[6 + (n * 4 + c // 4) % 2][:, 0:w * ROWS]).then_inc(list_ev, 1)

            keep_list(srcT, 0)
            over(act, CHUNKS, [(0, x_evac), (1, h_evac)])
            keep_list(relT, 1)
            keep_list(endT, 2)

            def distance(k, g, i):
                act.wait_ge(bc_in[0 if g < 7 else 1], i * 32 + 32)
                after(act, oh_ok, k - 1)
                nc.scalar.activation(SQ[ring(g)], bc[:, 0, g * CH:(g + 1) * CH], ACT.Square, bias=neg_p).then_inc(dist_ok, 1)

            def one_hot(k, g, i):
                act.wait_ge(dist_ok, k + 1)
                after(act, x_mm, k - 1)
                nc.scalar.activation(OH[ring(g)], SQ[ring(g)], ACT.Relu, bias=ones[:, 0:1], scale=-1.0).then_inc(oh_ok, 1)

            def relu(k, g, i):
                act.wait_ge(x_mm, k + 1)
                after(act, v_mm, k - 1)
                nc.scalar.activation(M1[ring(g)], bank[g % 2][:, :], ACT.Relu).then_inc(relu_ok, 1)

            def evac(k, g, i):
                act.wait_ge(s_tr, k + 1)
                after(act, o_mm, k - 1)
                nc.scalar.copy(STs[ring(g)], bank[4 + g % 2][:, :]).then_inc(st_ok, 1)

            groups(act, [(0, distance), (1, relu), (0, one_hot), (4, evac)])

            act.wait_ge(acc_ok, TILES)

            def bias_relu(h, p, w):
                after(act, n1_tr, h - 1)
                settle(act, "act")
                nc.scalar.activation(by_block(stg[p][:, :]), in_order(accT[:, ds(h * CH, CH)]), ACT.Relu, bias=B3).then_inc(n1_st, 1)

            over(act, CHUNKS, [(0, bias_relu)])
            act.wait_ge(stat_ok, 1)
            nc.scalar.activation(tmp[:, :], var[:, :], ACT.Sqrt, bias=eps[:, :]).then_inc(sq_ok, 1)

            def keep(h, p, w):
                act.wait_ge(nm_ok, h + 1)
                settle(act, "act")
                nc.scalar.copy(step_of(h), nrm[p]).then_inc(cp_ok, 1)

            def keep_t(h, p, w):
                act.wait_ge(n1_t2, h + 1)
                settle(act, "act")
                nc.scalar.copy(in_order(accT[:, ds(h * CH, CH)]), by_block(bank[2 + p][:, :])).then_inc(x1t_ok, 1)

            def keep_ld(h, p, w):
                act.wait_ge(ld_mm, h + 1)
                after(act, ld_put[p], (h - p) * 8)
                settle(act, "act")
                nc.scalar.activation(lrow[p], bank[4 + p][0:1, :], ACT.Identity, bias=BE[0:1, :]).then_inc(ldb_ok, 1)

            over(act, CHUNKS, [(0, keep), (0, keep_t), (1, keep_ld)])

            def near_square(q, s, c):
                i = 2 * q + c
                if c == 0:
                    act.wait_ge(near_in[s], (q - s) * 8 + 16)
                after(act, oh2_ok, i)
                nc.scalar.activation(SQ2, near[:, s, c * HC * T:(c + 1) * HC * T], ACT.Square, bias=neg_p).then_inc(sq2_a, 1)

            def near_hot(q, s, c):
                act.wait_ge(sq2_a, 2 * q + c + 1)
                after(act, z_ld, (q - 1) * SC + (c + 1) * HC)
                nc.scalar.activation(OH2[c], SQ2, ACT.Relu, bias=ones[:, 0:1], scale=-1.0).then_inc(oh2_ok, 1)

            def spread_windows(q, s):
                act.wait_ge(lw_tr, q + 1)
                after(act, z_ld, (q - 1) * SC)
                nc.scalar.copy(LWd[:, s, 0:SC * SC:SC + 1], bank[7][:, 64:64 + SC]).then_inc(lw_ok, 1)

            def weights(q, s, more):
                act.wait_ge(z_mm, q + 1)
                after(act, lg_ok, q)
                nc.scalar.mul(low[0:SC, :], bank[4 + s][0:SC, 0:T], SLOPE).then_inc(low_ok, 1)
                if more:
                    near_square(q + 1, 1 - s, 0)
                    near_hot(q + 1, 1 - s, 0)
                    spread_windows(q + 1, 1 - s)
                act.wait_ge(dif_ok, q + 1)
                after(act, ev_tr, q)
                nc.scalar.activation(exd[0:SC, :], dif[0:SC, :], ACT.Exp).then_inc(exp_ok, 1)
                act.wait_ge(ev_tr, q + 1)
                after(act, sum_ok, (q - 1) * SC)
                after(act, gs_ok, (q - 1) * SC)
                nc.scalar.copy(evr[:, s], bank[7][:, 0:2 * SC].rearrange("p (a t) -> p a t", a=2)).then_inc(ev_ok, 1)

            def scale_rows(q, s, j):
                t = q * SC + j
                u = (s * SC + j) % 4
                if j == 0:
                    act.wait_ge(ev_ok, q + 1)
                after(act, t_mm, t - 3)
                nc.scalar.activation(Gs[u], G[:, s * SC + j, 1:F + 1], ACT.Copy, scale=evr[:, s, 0, j:j + 1]).then_inc(gs_ok, 1)

            def second(i, last=False):
                for s in range(2):
                    q = i * 2 + s
                    more = not (last and s == 1)
                    weights(q, s, more)
                    for j in range(SC):
                        scale_rows(q, s, j)
                        if more and j == SC // 5:
                            near_square(q + 1, 1 - s, 1)
                        if more and j == 2 * (SC // 5):
                            near_hot(q + 1, 1 - s, 1)

            act.wait_ge(cleared, 3)
            spread_windows(0, 0)
            for c in range(2):
                near_square(0, 0, c)
                near_hot(0, 0, c)
            second(0)
            with act.Fori(1, PASSES - 1) as i:
                second(i)
            second(PASSES - 1, last=True)

            def spread_inv(c, p, w):
                act.wait_ge(c_mm, c + 1)
                after(act, y_ok, c - 1)
                nc.scalar.copy(rec[p][:, 0:w], bank[6 + p][:, 0:w]).then_inc(rec_ok, 1)

            def expo(c, p, w):
                act.wait_ge(mm_ok, c + 1)
                after(act, ctx_ok, c - 1)
                nc.scalar.activation(ex[p][:, 0:w], mn[p][:, 0:w], ACT.Exp).then_inc(ex_ok, 1)

            def relu1(c, p, w):
                act.wait_ge(h1_mm, c + 1)
                after(act, h2_mm, c - 1)
                nc.scalar.activation(h1[p][:, 0:w], bank[2 + p][:, 0:w], ACT.Relu, bias=BB1).then_inc(h1_ok, 1)

            def relu2(c, p, w):
                act.wait_ge(h2_mm, c + 1)
                settle(act, "act")
                nc.scalar.activation(H[:, ds(c * CH, w)], bank[4 + p][:, 0:w], ACT.Relu, bias=BB2).then_inc(h2_ok, 1)

            over(act, CHUNKS, [(0, spread_inv), (1, expo), (2, relu1), (3, relu2)], width=CH, tail=N - CHUNKS * CH)
            act.wait_ge(aff_ok, 2)
            nc.scalar.activation(scl[:, :], bnmv[:, 1:2], ACT.Sqrt, bias=eps[:, :]).then_inc(aff_ok, 1)
            act.wait_ge(aff_ok, 7)

            def affine(h, p, w):
                after(act, n2_tr, h - 1)
                settle(act, "act")
                nc.scalar.activation(by_block(stg[p][:, :]), in_order(H[:, ds(h * CH, CH)]), ACT.Identity, bias=shf[:, :], scale=scl[:, :]).then_inc(n2_st, 1)

            over(act, CHUNKS, [(0, affine)])
            act.wait_ge(stat2_ok, 1)
            nc.scalar.activation(tmp[:, :], var[:, :], ACT.Sqrt, bias=eps[:, :]).then_inc(sq2_ok, 1)

        @block.tensor
        def _(pe):
            pe.wait_ge(consts, 7)

            def tr_x(h, p, w):
                pe.wait_ge(x_st[p], h - p + 2)
                after(pe, xt_cp, h - 1)
                for b in range(SB):
                    last = nc.tensor.transpose(bank[p][:, b * 128:(b + 1) * 128], stg[p][:, b * 128:(b + 1) * 128], ident[:, :])
                last.then_inc(xt_tr, 1)

            def mm_h(h, p, w):
                pe.wait_ge(xt_cp, h + 1)
                after(pe, h_ev, h - 1)
                nc.tensor.matmul(bank[2 + p][:, :], W1s[:, :], xTs[p], start=True, stop=True).then_inc(h_mm, 1)

            def mm_pq(h, p, w):
                pe.wait_ge(h_ev, h + 1)
                after(pe, pq_ev, 2 * h - 2)
                for b in range(SB):
                    last = nc.tensor.matmul(bank[4 + 2 * p + b // 2][:, b % 2 * 256:(b % 2 + 1) * 256], hTs[p][:, b * 128:(b + 1) * 128],
                                            Wpq[:, :, :].rearrange("k a n -> k (a n)"), start=True, stop=True)
                last.then_inc(pq_mm, 1)

            def tr_list(of, n, need):
                pe.wait_ge(prep, need)
                for c in range(COLS):
                    u = n * 4 + c // 4
                    if c % 4 == 0:
                        after(pe, list_ev, u - 1)
                    nc.tensor.transpose(bank[6 + u % 2][:, c % 4 * ROWS:(c % 4 + 1) * ROWS], of[0:ROWS, c, :],
                                        ident[0:ROWS, 0:ROWS]).then_inc(list_tr, 1)

            tr_list(srcF, 0, 1)
            pe.wait_ge(weights_in, 16 * 18)
            pe.wait_ge(prep, 2)
            pe.wait_ge(list_ev, 4)
            over(pe, CHUNKS, [(0, tr_x), (1, mm_h), (2, mm_pq)])
            pe.wait_ge(pq_ev, 2 * STEPS)
            tr_list(rel, 1, 3)
            tr_list(relend, 2, 6)

            def pre(k, g, i):
                pe.wait_ge(landed[g], i * 64 + 64)
                pe.wait_ge(win_in[g], i * 64 + 64)
                pe.wait_ge(oh_ok, k + 1)
                after(pe, relu_ok, used2(k, g))
                for j in range(GT):
                    o = bank[g % 2][:, j * 128:(j + 1) * 128]
                    nc.tensor.matmul(o, G[:, g * GT + j, 0:F], ident[:, :], start=True, stop=False)
                    last = nc.tensor.matmul(o, Pwin[:, g * GT + j, :], OH[ring(g)][:, j * 128:(j + 1) * 128], start=False, stop=True)
                last.then_inc(x_mm, 1)

            def mm3(k, g, i):
                pe.wait_ge(relu_ok, k + 1)
                after(pe, scan_ok, used2(k, g))
                nc.tensor.matmul(bank[2 + g % 2][:, :], W3s[:, :], M1[ring(g)], start=True, stop=True).then_inc(v_mm, 1)

            def tr_s(k, g, i):
                pe.wait_ge(scan_ok, k + 1)
                after(pe, st_ok, used2(k, g))
                for j in range(GT):
                    last = nc.tensor.transpose(bank[4 + g % 2][:, j * 128:(j + 1) * 128], S[ring(g)][:, j * 128:(j + 1) * 128], ident[:, :])
                last.then_inc(s_tr, 1)

            def pick(k, g, i):
                pe.wait_ge(st_ok, k + 1)
                pe.wait_ge(eoh_ok, k + 1)
                after(pe, acc_ok, used2(k, g) * GT)
                for j in range(GT):
                    last = nc.tensor.matmul(bank[6 + g % 2][:, j * 128:(j + 1) * 128], STs[ring(g)][:, j * 128:(j + 1) * 128],
                                            EOH[ring(g)][:, j, :], start=True, stop=True)
                last.then_inc(o_mm, 1)

            groups(pe, [(0, pre), (1, mm3), (3, tr_s), (5, pick)])

            def tr_1(h, p, w):
                pe.wait_ge(n1_st, h + 1)
                after(pe, n1_add, h - 1)
                for b in range(SB):
                    last = nc.tensor.transpose(bank[p][:, b * 128:(b + 1) * 128], stg[p][:, b * 128:(b + 1) * 128], ident[:, :])
                last.then_inc(n1_tr, 1)

            over(pe, CHUNKS, [(0, tr_1)])

            def tr_2(h, p, w):
                pe.wait_ge(nm_ok, h + 1)
                after(pe, x1t_ok, h - 1)
                for b in range(SB):
                    last = nc.tensor.transpose(bank[2 + p][:, b * 128:(b + 1) * 128], nrm[p][:, b, :], ident[:, :])
                last.then_inc(n1_t2, 1)

            def mm_ld(h, p, w):
                pe.wait_ge(x1t_ok, h + 1)
                after(pe, ldb_ok, h - 1)
                settle(pe, "pe")
                nc.tensor.matmul(bank[4 + p][0:1, :], WDST, accT[:, ds(h * CH, CH)], start=True, stop=True).then_inc(ld_mm, 1)

            over(pe, CHUNKS, [(0, tr_2), (1, mm_ld)])

            def tr_windows(q, s):
                pe.wait_ge(lw_in[s], (q - s) * (8 * SC) + 16 * SC)
                after(pe, lw_ok, q)
                settle(pe, "pe")
                nc.tensor.transpose(bank[7][:, 64:64 + SC], LW[0:SC, s, :], ident[0:SC, 0:SC]).then_inc(lw_tr, 1)

            def dst_logit(q, s, j):
                if j == 0:
                    pe.wait_ge(lw_ok, q + 1)
                    after(pe, dif_ok, q - 1)
                if j % HC == 0:
                    pe.wait_ge(oh2_ok, 2 * q + j // HC + 1)
                nc.tensor.matmul(bank[4 + s][0:SC, 0:T], LWd[:, s, j * SC:(j + 1) * SC], OH2[j // HC][:, j % HC * T:(j % HC + 1) * T],
                                 start=(j == 0), stop=False).then_inc(z_ld, 1)

            def softmax_mm(i, s, more):
                q = i * 2 + s
                pe.wait_ge(rows_landed[s], (i + 1) * (16 * SC))
                nc.tensor.matmul(bank[4 + s][0:SC, 0:T], G[:, s * SC:(s + 1) * SC, F + 1], ident[:, :], start=False, stop=True).then_inc(z_mm, 1)
                pe.wait_ge(sc_ok, 3 * q + 1)
                after(pe, run_ok, 2 * q)
                settle(pe, "pe")
                nc.tensor.matmul(bank[6][0:1, 0:SC], fw[0:SC, T - 1:T], ident[0:SC, 0:SC], start=True, stop=True).then_inc(last_tr, 1)
                pe.wait_ge(run_ok, 2 * q + 2)
                after(pe, cr, 3 * q)
                settle(pe, "pe")
                nc.tensor.matmul(bank[6][0:SC, 64:65], run[0:1, s, 0:SC], ones[0:1, 0:1], start=True, stop=True).then_inc(run_tr, 1)
                if more:
                    tr_windows(q + 1, 1 - s)
                pe.wait_ge(exp_ok, q + 1)
                after(pe, ev_ok, q)
                settle(pe, "pe")
                nc.tensor.transpose(bank[7][:, 0:SC], exd[0:SC, 0:T], ident[0:SC, 0:SC])
                nc.tensor.matmul(bank[7][:, SC:2 * SC], exd[0:SC, T:T + 1].broadcast_to([SC, 128]), ident[0:SC, 0:SC],
                                 start=True, stop=True).then_inc(ev_tr, 1)

            def sums(q, s, j):
                t = q * SC + j
                u = (s * SC + j) % 4
                pe.wait_ge(gs_ok, t + 1)
                if j % HC == 0:
                    pe.wait_ge(eq_ok, 2 * q + j // HC + 1)
                after(pe, sum_ok, t - 3)
                nc.tensor.matmul(bank[u][:, 0:128], Gs[u], EQ[j // HC][:, j % HC, :], start=True, stop=True).then_inc(t_mm, 1)

            def second(i, last=False):
                for s in range(2):
                    q = i * 2 + s
                    more = not (last and s == 1)
                    softmax_mm(i, s, more)
                    if more:
                        for j in range(3):
                            dst_logit(q + 1, 1 - s, j)
                    for j in range(SC):
                        sums(q, s, j)
                        if more and j >= 3:
                            dst_logit(q + 1, 1 - s, j)

            tr_windows(0, 0)
            for j in range(SC):
                dst_logit(0, 0, j)
            second(0)
            with pe.Fori(1, PASSES - 1) as i:
                second(i)
            second(PASSES - 1, last=True)

            def mm_c(c, p, w):
                after(pe, y_ok, c - 1)
                after(pe, rec_ok, c - 1)
                nc.tensor.matmul(bank[p][:, 0:w], wprojs[:, :], cacc[:, ds(c * CH, w)], start=True, stop=True)
                nc.tensor.matmul(bank[6 + p][:, 0:w], ones[0:1, :], inv[:, ds(c * CH, w)], start=True, stop=True).then_inc(c_mm, 1)

            def mm_h1(c, p, w):
                pe.wait_ge(ctx_ok, c + 1)
                after(pe, h1_ok, c - 1)
                nc.tensor.matmul(bank[2 + p][:, 0:w], w1s[:, 0, :], ctxb[p][:, 0:w], start=True, stop=False)
                nc.tensor.matmul(bank[2 + p][:, 0:w], w1s[:, 1, :], accT[:, ds(c * CH, w)], start=False, stop=True).then_inc(h1_mm, 1)

            def mm_h2(c, p, w):
                pe.wait_ge(h1_ok, c + 1)
                after(pe, h2_ok, c - 1)
                nc.tensor.matmul(bank[4 + p][:, 0:w], w2s[:, :], h1[p][:, 0:w], start=True, stop=True).then_inc(h2_mm, 1)

            pe.wait_ge(sum_ok, TILES)
            pe.wait_ge(inv_in, 16)
            over(pe, CHUNKS, [(0, mm_c), (2, mm_h1), (3, mm_h2)], width=CH, tail=N - CHUNKS * CH)

            def tr_3(h, p, w):
                pe.wait_ge(n2_st, h + 1)
                after(pe, n2_add, h - 1)
                for b in range(SB):
                    last = nc.tensor.transpose(bank[p][:, b * 128:(b + 1) * 128], stg[p][:, b * 128:(b + 1) * 128], ident[:, :])
                last.then_inc(n2_tr, 1)

            over(pe, CHUNKS, [(0, tr_3)])

        @block.vector
        def _(dve):
            v = nc.vector
            done = [0]

            def chain(ins):
                done[0] += 1
                ins.then_inc(turns["dve"], 1)
                dve.wait_ge(turns["dve"], done[0])

            R = slice(0, ROWS)
            dve.wait_ge(lists_in, 16 * 8)
            v.tensor_copy(srcF[R], S0[R]).then_inc(prep, 1)
            dve.wait_ge(weights_in, 16 * 18)
            dve.wait_ge(consts, 7)
            v.tensor_copy(Wpq[:, 1, :], W2s[:, 1, :])
            v.tensor_tensor(wprojs[0:127, :], wprojs[0:127, :], wproj0[0:127, :], ALU.subtract)
            v.tensor_tensor(Wpq[:, 0, :], W2s[:, 0, :], W2s[:, 1, :], ALU.subtract).then_inc(prep, 1)

            def ev_pq(h, p, w):
                dve.wait_ge(pq_mm, h + 1)
                after(dve, pq_out[p], (h - p) * 16)
                for c in range(2):
                    v.tensor_tensor(pqs[p][:, 2 * c:2 * c + 2, :], bank[4 + 2 * p + c][:, :].rearrange("p (b n) -> p b n", b=2),
                                    brow[:, :, :].rearrange("p a n -> p (a n)").unsqueeze(1).broadcast_to([128, 2, 256]), ALU.add).then_inc(pq_ev, 1)

            dve.wait_ge(x_in, 16 * (STEPS + 1))
            over(dve, CHUNKS, [(0, stage(dve, v, 1)), (3, ev_pq)])
            here, before, next_ = D[R, :, 1:T + 1], D[R, :, 0:T], D[R, :, 2:T + 2]
            v.tensor_tensor(rel[R], here, D[R, :, 1:2].broadcast_to([ROWS, COLS, T]), ALU.subtract).then_inc(prep, 1)
            chain(v.tensor_tensor(flag[R], here, before, ALU.not_equal))
            dve.wait_ge(prep, 3)
            v.tensor_copy(metaS[R, 0], rel[R])
            v.tensor_scalar(metaS[R, 3], rel[R], 0.0, NEG, ALU.not_equal, ALU.mult)
            chain(v.tensor_scalar(metaS[R, 1], flag[R], NEG, None, ALU.mult))
            chain(v.tensor_scalar(contS[R, :], rel[R, :, T - 1:T].rearrange("p c e -> p (c e)"), 0.0, None, ALU.not_equal))
            v.scalar_tensor_tensor(out=contS[R, :], in0=contS[R, :], scalar=NEG, in1=metaS[R, 1, :, 0:1].rearrange("p c e -> p (c e)"),
                                   op0=ALU.mult, op1=ALU.add).then_inc(prep, 1)
            chain(v.tensor_tensor(flag[R], next_, here, ALU.not_equal))
            v.tensor_scalar(metaS[R, 2], flag[R], NEG, None, ALU.mult).then_inc(prep, 1)
            chain(v.scalar_tensor_tensor(out=relend[R], in0=rel[R], scalar=1.0, in1=flag[R], op0=ALU.add, op1=ALU.mult))
            chain(v.tensor_scalar(relend[R], relend[R], -1.0, None, ALU.add))
            v.engine_nop().then_inc(prep, 2)

            dve.wait_ge(list_ev, 12)
            dve.wait_ge(rows_in, 16)
            dve.wait_ge(base_in, 32)
            dve.wait_ge(cleared, 1)

            at = {}

            def scan(k, g, i):
                dve.wait_ge(v_mm, k + 1)
                after(dve, s_tr, k - 1)
                after(dve, scan_ok, k)
                first = isinstance(k, int) and k == 0
                v.tensor_tensor_scan(out=S[ring(g)], data0=bc[:, 1, g * CH:(g + 1) * CH], data1=bank[2 + g % 2][:, :],
                                     initial=NEG if first else S[ring((g - 1) % GROUPS)][:, CH - 1:CH], op0=ALU.add, op1=ALU.max).then_inc(scan_ok, 1)

            def ends(k, g, i):
                after(dve, o_mm, k - 1)
                v.tensor_tensor(EOH[ring(g)], iota_n[:, :].unsqueeze(1).broadcast_to([128, GT, 128]),
                                endT[:, ds(k * GT, GT)].unsqueeze(2).broadcast_to([128, GT, 128]), ALU.is_equal).then_inc(eoh_ok, 1)

            def add_up(j):
                def f(k, g, i):
                    if j == 0:
                        at[0] = bases(mybir.EngineType.DVE, k * GT, GT)
                    win = accT[:, ds(at[0][j], 128)]
                    if j == 0:
                        dve.wait_ge(o_mm, k + 1)
                    after(dve, acc_ok, k * GT + j)
                    v.tensor_tensor(win, win, bank[6 + g % 2][:, j * 128:(j + 1) * 128], ALU.add).then_inc(acc_ok, 1)
                return f

            groups(dve, [(6, add_up(0)), (2, scan), (6, add_up(1)), (4, ends), (6, add_up(2)), (6, add_up(3))])

            def add_to_x(sem_tr, sem_add):
                def f(h, p, w):
                    dve.wait_ge(sem_tr, h + 1)
                    xs = step_of(h)
                    v.tensor_tensor(xs, xs, bank[p][:, :].rearrange("p (b f) -> p b f", b=SB), ALU.add).then_inc(sem_add, 1)
                return f

            def row_stats(sem_add, sem_bn):
                def f(h, p, w):
                    dve.wait_ge(sem_add, h + 1)
                    settle(dve, "dve_waits")
                    for b in range(SB):
                        v.bn_stats(stats[:, ds(h * SB + b, 1), :].rearrange("p a b -> p (a b)"), block_of(h, b)).then_inc(sem_bn, 1)
                return f

            def moments(sem_bn, ready):
                dve.wait_ge(sem_bn, BLOCKS)
                me, ve, mo, vo = (stats[:, :, k] for k in (1, 2, 4, 5))
                chain(v.tensor_tensor(tmp[:, :], me, mo, ALU.subtract))
                chain(v.tensor_tensor(mean[:, :], me, mo, ALU.add))
                chain(v.tensor_tensor(var[:, :], ve, vo, ALU.add))
                chain(v.tensor_tensor(tmp[:, :], tmp[:, :], tmp[:, :], ALU.mult))
                chain(v.tensor_scalar(mean[:, :], mean[:, :], 0.5, None, ALU.mult))
                chain(v.tensor_scalar(tmp[:, :], tmp[:, :], 0.25, None, ALU.mult))
                v.scalar_tensor_tensor(out=var[:, :], in0=var[:, :], scalar=1.0 / F, in1=tmp[:, :], op0=ALU.mult, op1=ALU.add).then_inc(ready, 1)

            def scales(sq):
                dve.wait_ge(sq, 1)
                chain(v.reciprocal(rstd[:, :], tmp[:, :]))
                chain(v.scalar_tensor_tensor(out=nmr[:, :], in0=mean[:, :], scalar=-1.0, in1=rstd[:, :], op0=ALU.mult, op1=ALU.mult))

            dve.wait_ge(x_in, 16 * (STEPS + 1))
            over(dve, CHUNKS, [(0, add_to_x(n1_tr, n1_add)), (1, row_stats(n1_add, n1_bn))])
            moments(n1_bn, stat_ok)
            scales(sq_ok)

            def scale_step(done, scaled):
                def f(h, p, w):
                    after(dve, done, h - 1)
                    v.tensor_tensor(stg[p][:, :].rearrange("p (b f) -> p b f", b=SB), step_of(h),
                                    rstd[:, ds(h * SB, SB)].unsqueeze(2).broadcast_to([128, SB, F]), ALU.mult).then_inc(scaled, 1)
                return f

            def shifted(p, h, to):
                return v.tensor_tensor(to, stg[p][:, :].rearrange("p (b f) -> p b f", b=SB),
                                       nmr[:, ds(h * SB, SB)].unsqueeze(2).broadcast_to([128, SB, F]), ALU.add)

            def shift_step(h, p, w):
                dve.wait_ge(sc1_ok, h + 1)
                after(dve, cp_ok, h - 1)
                after(dve, n1_t2, h - 1)
                after(dve, lp_ok, h - 1)
                shifted(p, h, nrm[p]).then_inc(nm_ok, 1)

            def src_logit(h, p, w):
                dve.wait_ge(lp_ok, h + 1)
                v.tensor_reduce(out=X[:, ds(h * SB, SB), F + 1:F + 2].rearrange("p a b -> p (a b)"), in_=lprod[p],
                                axis=mybir.AxisListType.X, op=ALU.add).then_inc(ls_ok, 1)

            over(dve, CHUNKS, [(0, scale_step(nm_ok, sc1_ok)), (1, shift_step), (3, src_logit)])

            def softmax(i, s):
                q = i * 2 + s
                logits = bank[4 + s][0:SC, 0:T]
                starts, finishes, others = (mts[s][0:SC, k, :] for k in range(3))
                dve.wait_ge(low_ok, q + 1)
                after(dve, dif_ok, q)
                v.tensor_tensor(lg[0:SC, :], logits, low[0:SC, :], ALU.max).then_inc(lg_ok, 1)
                dve.wait_ge(lg_ok, q + 1)
                dve.wait_ge(meta_in[s], i * 16 + 16)
                after(dve, last_tr, q)
                v.tensor_tensor_scan(out=fw[0:SC, :], data0=starts, data1=lg[0:SC, :], initial=NEG, op0=ALU.add, op1=ALU.max).then_inc(sc_ok, 1)
                v.tensor_tensor_scan(out=bk[0:SC, ::-1], data0=finishes[:, ::-1], data1=lg[0:SC, ::-1], initial=NEG, op0=ALU.add, op1=ALU.max).then_inc(sc_ok, 1)
                after(dve, run_tr, q - 1)
                v.tensor_copy(run[0:1, s, 0:1], run[0:1, 1 - s, SC:SC + 1]).then_inc(run_ok, 1)
                dve.wait_ge(last_tr, q + 1)
                dve.wait_ge(run_ok, 2 * q + 1)
                v.tensor_tensor_scan(out=run[0:1, s, 1:SC + 1], data0=cont[:, ds(q * SC, SC)], data1=bank[6][0:1, 0:SC],
                                     initial=run[0:1, s, 0:1], op0=ALU.add, op1=ALU.max).then_inc(run_ok, 1)
                dve.wait_ge(sc_ok, 3 * q + 2)
                v.tensor_tensor(mM[0:SC, :], fw[0:SC, :], bk[0:SC, :], ALU.max).then_inc(sc_ok, 1)
                dve.wait_ge(run_tr, q + 1)
                v.tensor_tensor(carry[0:SC, :], bank[6][0:SC, 64:65], starts[:, 0:1], ALU.add).then_inc(cr, 1)
                dve.wait_ge(cr, 3 * q + 1)
                dve.wait_ge(sc_ok, 3 * q + 3)
                v.scalar_tensor_tensor(out=mM[0:SC, :], in0=others, scalar=carry[0:SC, :], in1=mM[0:SC, :], op0=ALU.add, op1=ALU.max).then_inc(cr, 1)
                dve.wait_ge(cr, 3 * q + 2)
                after(dve, exp_ok, q)
                v.tensor_tensor(dif[0:SC, T:T + 1], carry[0:SC, :], mM[0:SC, 0:1], ALU.subtract).then_inc(cr, 1)
                dve.wait_ge(cr, 3 * q + 3)
                v.tensor_tensor(dif[0:SC, 0:T], lg[0:SC, :], mM[0:SC, :], ALU.subtract).then_inc(dif_ok, 1)

            def columns(q, c):
                after(dve, t_mm, (q - 1) * SC + (c + 1) * HC)
                v.tensor_tensor(EQ[c], iota_n[:, :].unsqueeze(1).broadcast_to([128, HC, 128]),
                                relT[:, ds(q * SC + c * HC, HC)].unsqueeze(2).broadcast_to([128, HC, 128]), ALU.is_equal).then_inc(eq_ok, 1)

            def sum_up(q, s, j, at):
                t = q * SC + j
                win = cacc[:, ds(at[j % LD], 128)]
                dve.wait_ge(t_mm, t + 1)
                after(dve, sum_ok, t)
                v.scalar_tensor_tensor(out=win, in0=win, scalar=evr[:, s, 1, j:j + 1], in1=bank[(s * SC + j) % 4][:, 0:128],
                                       op0=ALU.mult, op1=ALU.add).then_inc(sum_ok, 1)

            def second(i):
                for s in range(2):
                    q = i * 2 + s
                    softmax(i, s)
                    columns(q, 0)
                    for j in range(SC):
                        if j % LD == 0:
                            here = bases(mybir.EngineType.DVE, q * SC + j, LD)
                        sum_up(q, s, j, here)
                        if j == 1:
                            columns(q, 1)

            dve.wait_ge(ls_ok, STEPS)
            dve.wait_ge(cleared, 2)
            second(0)
            with dve.Fori(1, PASSES) as i:
                second(i)

            def ratio(c, p, w):
                dve.wait_ge(c_mm, c + 1)
                dve.wait_ge(rec_ok, c + 1)
                after(dve, mm_ok, c - 1)
                v.tensor_tensor(Y[p][:, 0:w], bank[p][:, 0:w], rec[p][:, 0:w], ALU.mult).then_inc(y_ok, 1)

            def signs(c, p, w):
                dve.wait_ge(y_ok, c + 1)
                after(dve, ctx_ok, c - 1)
                v.tensor_scalar(mx[p][:, 0:w], Y[p][:, 0:w], 0.0, None, ALU.max)
                v.tensor_scalar(mn[p][:, 0:w], Y[p][:, 0:w], 0.0, None, ALU.min).then_inc(mm_ok, 1)

            def elu(c, p, w):
                dve.wait_ge(ex_ok, c + 1)
                dve.wait_ge(mm_ok, c + 1)
                after(dve, h1_mm, c - 1)
                v.scalar_tensor_tensor(out=ctxb[p][:, 0:w], in0=ex[p][:, 0:w], scalar=-1.0, in1=mx[p][:, 0:w], op0=ALU.add, op1=ALU.add).then_inc(ctx_ok, 1)

            def col_stats(c, p, w):
                dve.wait_ge(h2_ok, c + 1)
                settle(dve, "dve_waits")
                v.bn_stats(bnst[:, ds(c, 1), :].rearrange("p a b -> p (a b)"), H[:, ds(c * CH, w)]).then_inc(bn_ok, 1)

            dve.wait_ge(den_in, 16)
            v.reciprocal(dens[0:RP, :], dens[0:RP, :]).then_inc(inv_ok, 1)
            over(dve, CHUNKS, [(0, ratio), (0, signs), (1, elu), (4, col_stats)], width=CH, tail=N - CHUNKS * CH)
            dve.wait_ge(bn_ok, CHUNKS + 1)
            v.bn_aggr(bnmv[:, :], bnst[:, :, :].rearrange("p a b -> p (a b)")).then_inc(aff_ok, 2)
            dve.wait_ge(aff_ok, 3)
            v.reciprocal(scl[:, :], scl[:, :]).then_inc(aff_ok, 1)
            dve.wait_ge(aff_ok, 4)
            v.tensor_tensor(scl[:, :], scl[:, :], GAM, ALU.mult).then_inc(aff_ok, 1)
            dve.wait_ge(aff_ok, 5)
            v.scalar_tensor_tensor(out=shf[:, :], in0=bnmv[:, 0:1], scalar=-1.0, in1=scl[:, :], op0=ALU.mult, op1=ALU.mult).then_inc(aff_ok, 1)
            dve.wait_ge(aff_ok, 6)
            v.tensor_tensor(shf[:, :], shf[:, :], BET, ALU.add).then_inc(aff_ok, 1)

            over(dve, CHUNKS, [(0, add_to_x(n2_tr, n2_add)), (1, row_stats(n2_add, n2_bn))])
            moments(n2_bn, stat2_ok)
            scales(sq2_ok)

            def finish(h, p, w):
                dve.wait_ge(sc2_ok, h + 1)
                after(dve, out_done[p], (h - p) * 8)
                shifted(p, h, outs[p]).then_inc(nm2_ok, 1)

            over(dve, CHUNKS, [(0, scale_step(nm2_ok, sc2_ok)), (1, finish)])


_INS = ['x', 'src', 'dst', 'L0_gnn_W1', 'L0_gnn_b1', 'L0_gnn_W2', 'L0_gnn_b2', 'L0_gnn_W3', 'L0_gnn_b3',
        'L1_gnn_we_dst', 'L1_gnn_we_src', 'L1_gnn_be', 'L1_gnn_w_proj', 'L1_gnn_b_proj', 'L1_gnn_w1', 'L1_gnn_b1',
        'L1_gnn_w2', 'L1_gnn_b2', 'L1_gnn_gamma', 'L1_gnn_beta']


def kernel(**inputs):
    import numpy as _np
    import concourse.bacc as _bacc
    from concourse import mybir as _mybir
    from concourse.bass_utils import run_bass_kernel_spmd as _run

    nc = _bacc.Bacc("TRN2", target_bir_lowering=False, num_devices=1)
    arrays, args = {}, []
    for name in _INS:
        a = _np.ascontiguousarray(inputs[name])
        arrays[f"in_{name}"] = a
        args.append(nc.dram_tensor(f"in_{name}", a.shape, _mybir.dt.from_np(a.dtype), kind="ExternalInput").ap())
    args.append(nc.dram_tensor("out_0", (N, F), _mybir.dt.float32, kind="ExternalOutput").ap())
    build(nc, *args)
    r = _run(nc, [arrays], core_ids=[0])
    return r.results[0]["out_0"]
```
